# Optimizing a Trainium2 kernel written in Bass

```python
import numpy as np
import jax
import jax.numpy as jnp

def _softmax(x, axis=-1):
    return jax.nn.softmax(x, axis=axis)

def _gelu(x):
    return jax.nn.gelu(x, approximate=True)

def _silu(x):
    return jax.nn.silu(x)

def _sigmoid(x):
    return jax.nn.sigmoid(x)

def _layernorm(x, axis=-1, eps=1e-05):
    m = jnp.mean(x, axis=axis, keepdims=True)
    v = jnp.var(x, axis=axis, keepdims=True)
    return (x - m) / jnp.sqrt(v + eps)

def _scatter_add(tgt, idx, src, axis=0):
    return tgt.at[idx].add(src)

def _segment_sum(src, seg, n):
    return jax.ops.segment_sum(src, seg, n)
kernel_name = 'mk_audio_tower_d1_tok_audfeat512_r4_9f6b36'

def setup_inputs(seed: int=0):
    np.random.seed(seed)
    _w = jnp.asarray

    def _rec_inputs():
        import jax
        import jax.numpy as jnp
        _rk = jax.random.key(seed)
        x = -0.000392918 + 0.999932 * jax.random.normal(jax.random.fold_in(_rk, 1), (32, 256, 128), jnp.float32)
        return x
    x = _rec_inputs()

    def _L0_tok_setup():
        import jax, jax.numpy as jnp
        import numpy as np
        CHANNELS = 128
        KERNEL = 7
        NORM_FACTOR = 1.0
        SQUEEZE = 1
        key = jax.random.key(seed)
        kx, kw = jax.random.split(key)
        B, T, C = (8, 1024, CHANNELS)
        x = jax.random.normal(kx, (B, T, C), dtype=jnp.float32)
        fan_in = C * KERNEL
        weights = jax.random.normal(kw, (C // SQUEEZE, C, KERNEL), dtype=jnp.float32) / jnp.sqrt(jnp.float32(fan_in))
        return {'x': x, 'weights': weights}
    _L0_tok_all = _L0_tok_setup()
    _L0_tok_in = {k: v for k, v in _L0_tok_all.items() if k in ('weights',)}
    del _L0_tok_all

    def _L0_attn_setup():
        import jax, jax.numpy as jnp
        import numpy as np
        B, T, D, K, V = (4, 1024, 128, 128, 128)
        key = jax.random.key(seed)
        ks = jax.random.split(key, 7)
        w = lambda k, shp: jax.random.normal(k, shp, dtype=jnp.float32) * 0.02
        return {'minibatch': jax.random.normal(ks[0], (B, T, D), dtype=jnp.float32), 'Wk': w(ks[1], (D, K)), 'bk': jnp.zeros((K,), jnp.float32), 'Wq': w(ks[2], (D, K)), 'bq': jnp.zeros((K,), jnp.float32), 'Wv': w(ks[3], (D, V)), 'bv': jnp.zeros((V,), jnp.float32)}
    _L0_attn_all = _L0_attn_setup()
    _L0_attn_in = {k: v for k, v in _L0_attn_all.items() if k in ('Wk', 'bk', 'Wq', 'bq', 'Wv', 'bv')}
    del _L0_attn_all

    def _L0_ffn_setup():
        import jax, jax.numpy as jnp
        import numpy as np
        B, N, D, E = (8, 2048, 128, 8)
        H = 2 * D
        key = jax.random.key(seed)
        ks = jax.random.split(key, 7)
        s = 0.02
        return {'x': jax.random.normal(ks[0], (B, N, D), dtype=jnp.float32), 'W1': jax.random.normal(ks[1], (E, D, H), dtype=jnp.float32) * s, 'b1': jnp.zeros((E, H), dtype=jnp.float32), 'W2': jax.random.normal(ks[2], (E, H, D), dtype=jnp.float32) * s, 'b2': jnp.zeros((E, D), dtype=jnp.float32), 'Wg': jax.random.normal(ks[3], (D, E), dtype=jnp.float32) * s, 'bg': jnp.zeros((E,), dtype=jnp.float32)}
    _L0_ffn_all = _L0_ffn_setup()
    _L0_ffn_in = {k: v for k, v in _L0_ffn_all.items() if k in ('W1', 'b1', 'W2', 'b2', 'Wg', 'bg')}
    del _L0_ffn_all
    return {'x': x, 'L0_tok_weights': _L0_tok_in['weights'], 'L0_attn_Wk': _L0_attn_in['Wk'], 'L0_attn_bk': _L0_attn_in['bk'], 'L0_attn_Wq': _L0_attn_in['Wq'], 'L0_attn_bq': _L0_attn_in['bq'], 'L0_attn_Wv': _L0_attn_in['Wv'], 'L0_attn_bv': _L0_attn_in['bv'], 'L0_ffn_W1': _L0_ffn_in['W1'], 'L0_ffn_b1': _L0_ffn_in['b1'], 'L0_ffn_W2': _L0_ffn_in['W2'], 'L0_ffn_b2': _L0_ffn_in['b2'], 'L0_ffn_Wg': _L0_ffn_in['Wg'], 'L0_ffn_bg': _L0_ffn_in['bg']}

def reference(x, L0_tok_weights, L0_attn_Wk, L0_attn_bk, L0_attn_Wq, L0_attn_bq, L0_attn_Wv, L0_attn_bv, L0_ffn_W1, L0_ffn_b1, L0_ffn_W2, L0_ffn_b2, L0_ffn_Wg, L0_ffn_bg):
    import jax
    import jax.numpy as jnp

    def _L0_tok_ref(x, weights):
        import jax, jax.numpy as jnp
        import numpy as np
        CHANNELS = 128
        KERNEL = 7
        NORM_FACTOR = 1.0
        SQUEEZE = 1
        B, T, C = x.shape
        K = KERNEL
        patches = jax.lax.conv_general_dilated_patches(jnp.transpose(x, (0, 2, 1)), filter_shape=(K,), window_strides=(1,), padding=((0, 0),))
        L = patches.shape[-1]
        xu = jnp.transpose(patches.reshape(B, C, K, L), (0, 2, 1, 3))
        w = jnp.einsum('blc,dck->bkdl', x[:, -L:, :], weights)
        w = jnp.tanh(w / NORM_FACTOR)
        w = jnp.repeat(w, repeats=SQUEEZE, axis=2)
        out = jnp.sum(xu * w, axis=1)
        return jnp.transpose(out, (0, 2, 1))

    def _L0_attn_ref(minibatch, Wk, bk, Wq, bq, Wv, bv):
        import jax, jax.numpy as jnp
        import numpy as np
        B, T, D, K, V = (4, 1024, 128, 128, 128)
        keys = minibatch @ Wk + bk
        queries = minibatch @ Wq + bq
        values = minibatch @ Wv + bv
        logits = jnp.einsum('btk,bsk->bts', queries, keys)
        t = logits.shape[1]
        mask = jnp.triu(jnp.ones((t, t), dtype=bool), k=1)
        logits = jnp.where(mask[None, :, :], -jnp.inf, logits)
        sqrt_k = jnp.asarray(np.sqrt(K), dtype=logits.dtype)
        probs = jax.nn.softmax(logits, axis=1) / sqrt_k
        read = jnp.einsum('bts,bsv->btv', probs, values)
        return minibatch + read

    def _L0_ffn_ref(x, W1, b1, W2, b2, Wg, bg):
        import jax, jax.numpy as jnp
        import numpy as np
        B, N, D, E = (8, 2048, 128, 8)
        H = 2 * D
        Bs, Ns, Ds = x.shape
        xf = x.reshape(Bs * Ns, Ds)
        logits = xf @ Wg + bg
        idx = jnp.argmax(logits, axis=-1)
        out = jnp.zeros_like(xf)
        num_experts = W1.shape[0]
        for e in range(num_experts):
            h = jax.nn.relu(xf @ W1[e] + b1[e])
            y = h @ W2[e] + b2[e]
            out = jnp.where((idx == e)[:, None], y, out)
        return out.reshape(Bs, Ns, Ds)
    h = _L0_tok_ref(x, L0_tok_weights)
    h = h + _L0_attn_ref(_layernorm(h, axis=-1), L0_attn_Wk, L0_attn_bk, L0_attn_Wq, L0_attn_bq, L0_attn_Wv, L0_attn_bv)
    h = h + _L0_ffn_ref(_layernorm(h, axis=-1), L0_ffn_W1, L0_ffn_b1, L0_ffn_W2, L0_ffn_b2, L0_ffn_Wg, L0_ffn_bg)
    return h

_drawn_inputs = setup_inputs


def setup_inputs(seed=0):
    import zlib

    import numpy as np

    out = dict(_drawn_inputs(seed))
    spreads = {'L0_attn_bk': (0.0, 0.8),
     'L0_attn_bq': (0.0, 0.8),
     'L0_attn_bv': (0.0, 0.8),
     'L0_ffn_b1': (0.0, 0.662),
     'L0_ffn_b2': (0.0, 0.1),
     'L0_ffn_bg': (0.0, 0.1)}
    factors = {'L0_attn_Wk': 8.0, 'L0_attn_Wq': 8.0, 'L0_attn_Wv': 8.0}
    for name, (base, spread) in spreads.items():
        noise = np.random.default_rng([zlib.crc32(name.encode()), seed]).standard_normal(out[name].shape)
        drawn = base * np.exp(spread * noise) if base else spread * noise
        out[name] = jnp.asarray(drawn.astype(out[name].dtype))
    for name, factor in factors.items():
        out[name] = (out[name] * factor).astype(out[name].dtype)
    return out
```

```python
from contextlib import ExitStack

import concourse.bass as bass
from concourse import mybir

FP32 = mybir.dt.float32
BF16 = mybir.dt.bfloat16
INT32 = mybir.dt.int32
UINT32 = mybir.dt.uint32
ALU = mybir.AluOpType
ACT = mybir.ActivationFunctionType
AX = mybir.AxisListType

MASKED = -1.0e30
EPS = 1e-5


class Turn:

    def __init__(self, loop, times, offset):
        self.loop, self.times, self.offset = loop, times, offset

    def __add__(self, n):
        return Turn(self.loop, self.times, self.offset + n)

    @property
    def slot(self):
        return self.offset % self.times

    def count(self, per, extra=0):
        return self.loop * (self.times * per) + (self.offset * per + extra)

    def rounds(self, per, extra=0):
        return self.loop * per + (self.offset // self.times * per + extra)

    def at_least(self, n):
        return not isinstance(self.loop, int) or self.offset >= n


def audio_tower(nc, x, tok_w, wk, bk, wq, bq, wv, bv, w1, b1, w2, b2, wg, bg, out):
    B, TX, D = x.shape
    TAPS = tok_w.shape[2]
    L = TX - TAPS + 1
    E, _, H = w1.shape
    N = B * L
    PER = 2
    GROUPS = B // PER
    HALF = L // 2
    TILES = 2 * PER
    GT = PER * L
    HC = H // 128
    REGION = -(-N // 128) * 128 + 128
    PADDING = E * REGION
    ROW = D + 3
    MEAN, RSTD, TOKEN = D, D + 1, D + 2
    SLOTS = (N + E * 127) // 128
    NOWHERE = 1.0e6
    READ_SCALE = float(D) ** -0.5
    BANKS = 3

    x_rows = x.rearrange("b t c -> (b t) c")
    out_rows = out.rearrange("b t c -> (b t) c")
    routed = nc.dram_tensor("routed", (PADDING + 128, ROW), FP32).ap()

    ctx = ExitStack()
    with ctx:
        def sb(name, shape, dt=FP32):
            return ctx.enter_context(nc.sbuf_tensor(name, shape, dt))

        def pb(name):
            return ctx.enter_context(nc.psum_tensor(name, [128, 512], FP32))

        def sem(name):
            return ctx.enter_context(nc.semaphore(name))

        ident = sb("ident", [128, 128])
        ident_bf = sb("ident_bf", [128, 128], BF16)
        mask_bf = sb("mask_bf", [128, HALF], BF16)
        before_bf = sb("before_bf", [128, HALF], BF16)
        ones_bf = sb("ones_bf", [128, 128], BF16)
        tokw_raw = sb("tokw_raw", [128, D * TAPS])
        tokw = sb("tokw", [128, TAPS, D])
        wq_s = sb("wq_s", [128, D])
        wk_s = sb("wk_s", [128, D])
        wv_s = sb("wv_s", [128, D])
        bq_s = sb("bq_s", [128, 1])
        bk_s = sb("bk_s", [128, 1])
        bv_s = sb("bv_s", [128, D])
        wg_s = sb("wg_s", [128, E])
        bg_s = sb("bg_s", [128, E])
        w1_s = sb("w1_s", [128, E, H])
        w2_s = sb("w2_s", [128, E, HC, D])
        b1_s = sb("b1_s", [128, E, H])
        b2_s = sb("b2_s", [128, E, ROW])
        eps_s = sb("eps_s", [128, TILES])
        power_s = sb("power_s", [128, TILES])
        zero_s = sb("zero_s", [128, TILES])
        ramp = sb("ramp", [128, E])
        next_token = sb("next_token", [128, TILES])
        group_step = sb("group_step", [128, TILES])
        base = sb("base", [128, E])
        padding_rows = sb("padding_rows", [128, ROW])

        x_in = sb("x_in", [128, 2, 4, 128])
        xT = sb("xT", [128, 2, PER, TX])
        prod = sb("prod", [128, TAPS, GT])
        hT = sb("hT", [128, TILES, HALF])
        stats1 = sb("stats1", [128, TILES, 6])
        moments1 = sb("moments1", [128, TILES, 2])
        m = sb("m", [128, TILES, 128])
        hm = sb("hm", [128, TILES, 128])
        mT = sb("mT", [128, TILES, HALF])
        qT = sb("qT", [128, PER, L])
        kT = sb("kT", [128, PER, L])
        vb = sb("vb", [128, TILES, 128])
        vs = sb("vs", [128, TILES, 128])
        neg_max = sb("neg_max", [128, TILES])
        den = sb("den", [128, TILES])
        rden = sb("rden", [128, TILES])
        probs = sb("probs", [128, PER, L + HALF])
        rows = sb("rows", [128, 2, TILES, ROW])
        stats2 = sb("stats2", [128, TILES, 6])
        xf = sb("xf", [128, TILES, 128])
        xfT = sb("xfT", [128, TILES, HALF])
        logits = sb("logits", [128, TILES, E])
        top = sb("top", [128, TILES])
        is_top = sb("is_top", [128, TILES, E])
        top_ramp = sb("top_ramp", [128, TILES, E])
        first = sb("first", [128, TILES])
        onehot = sb("onehot", [128, TILES, E], BF16)
        place = sb("place", [128, TILES, E])
        place1 = sb("place1", [128, TILES, E])
        row_sum = sb("row_sum", [128, TILES])
        row_at = sb("row_at", [128, 2, TILES], UINT32)

        region_at = sb("region_at", [1, E])
        row_end = sb("row_end", [1, E], INT32)
        held = sb("held", [1, E], INT32)
        held_up = sb("held_up", [1, E], INT32)
        tiles_i = sb("tiles_i", [1, E], INT32)
        tiles_f = sb("tiles_f", [1, E])
        ones_e = sb("ones_e", [1, E])
        tile_end = sb("tile_end", [1, E])
        tile_start = sb("tile_start", [1, E])
        shift_e = sb("shift_e", [1, E])
        slot_no = sb("slot_no", [1, SLOTS, E])
        slot_row = sb("slot_row", [1, SLOTS, E])
        begun = sb("begun", [1, SLOTS, E])
        ended = sb("ended", [1, SLOTS, E])
        at_e = sb("at_e", [1, SLOTS, E])
        table_f = sb("table_f", [1, 2, SLOTS])
        table = sb("table", [1, 2, SLOTS], INT32)

        tl = sb("tl", [128, 4, ROW])
        xs = sb("xs", [128, 2, 128])
        xsT = sb("xsT", [128, 2, 128])
        hid = sb("hid", [128, 2, H])
        hidT = sb("hidT", [128, 2, H])
        res = sb("res", [128, 4, ROW])
        token_at = sb("token_at", [128, 4], UINT32)
        done_rows = sb("done_rows", [128, 4, 128])

        conv_bank = [pb(f"conv_bank{i}") for i in range(BANKS)]
        turn_bank = pb("turn_bank")
        h_bank = pb("h_bank")
        k_bank = pb("k_bank")
        q_bank = pb("q_bank")
        gate_bank = pb("gate_bank")
        score_bank = [q_bank, k_bank]
        gate_out = gate_bank[0:HALF, 0:TILES * E].rearrange("p (j e) -> p j e", e=E)
        rank_out = gate_bank[0:HALF, 64:64 + TILES * E].rearrange("p (j e) -> p j e", e=E)
        total_out = gate_bank[0:HALF, 128:128 + E]

        hid_bank = [conv_bank[2], turn_bank]
        hidT_bank = [h_bank, k_bank]
        y_bank = [q_bank, gate_bank]

        def tiles_of(bank, n=TILES):
            return bank[0:HALF, 0:n * 128].rearrange("p (j c) -> p j c", c=128)

        weights_in = sem("weights_in")
        late_in = sem("late_in")
        consts_made = sem("consts_made")
        const_steps = sem("const_steps")
        tokw_turned = sem("tokw_turned")
        tokw_ready = sem("tokw_ready")
        x_loaded = [sem(f"x_loaded{i}") for i in range(2)]
        x_turned = sem("x_turned")
        xT_ready = sem("xT_ready")
        conv_mm = sem("conv_mm")
        conv_tanh = sem("conv_tanh")
        conv_mul = sem("conv_mul")
        pool_sum = sem("pool_sum")
        vector_sum = sem("vector_sum")
        h_ready = sem("h_ready")
        h_turned = sem("h_turned")
        stats1_ready = sem("stats1_ready")
        moments1_ready = sem("moments1_ready")
        var1_ready = sem("var1_ready")
        rstd1_ready = sem("rstd1_ready")
        m_ready = sem("m_ready")
        hm_ready = sem("hm_ready")
        m_turned = sem("m_turned")
        mT_ready = sem("mT_ready")
        q_mm = sem("q_mm")
        k_mm = sem("k_mm")
        v_mm = sem("v_mm")
        q_ready = sem("q_ready")
        k_ready = sem("k_ready")
        v_ready = sem("v_ready")
        scores_mm = sem("scores_mm")
        max_ready = sem("max_ready")
        probs_ready = sem("probs_ready")
        rden_ready = sem("rden_ready")
        vs_ready = sem("vs_ready")
        read_mm = sem("read_mm")
        h2_ready = sem("h2_ready")
        stats2_ready = sem("stats2_ready")
        moments2_ready = sem("moments2_ready")
        var2_ready = sem("var2_ready")
        rstd2_ready = sem("rstd2_ready")
        xf_ready = sem("xf_ready")
        xf_turned = sem("xf_turned")
        xfT_ready = sem("xfT_ready")
        gate_mm = sem("gate_mm")
        choice_steps = sem("choice_steps")
        onehot_ready = sem("onehot_ready")
        rank_mm = sem("rank_mm")
        place_steps = sem("place_steps")
        base_ready = sem("base_ready")
        place_ready = sem("place_ready")
        token_written = sem("token_written")
        token_next = sem("token_next")
        routed_out = [sem(f"routed_out{i}") for i in range(2)]
        padding_made = sem("padding_made")
        padding_out = sem("padding_out")
        table_steps = sem("table_steps")
        ends_ready = sem("ends_ready")
        table_ready = sem("table_ready")
        slot_loaded = [sem(f"slot_loaded{i}") for i in range(4)]
        xs_ready = sem("xs_ready")
        res_ready = sem("res_ready")
        xs_turned = sem("xs_turned")
        xsT_ready = sem("xsT_ready")
        layer1_mm = sem("layer1_mm")
        hid_ready = sem("hid_ready")
        hid_turned = sem("hid_turned")
        hidT_ready = sem("hidT_ready")
        layer2_mm = sem("layer2_mm")
        done_ready = sem("done_ready")
        done_out = [sem(f"done_out{i}") for i in range(4)]

        block = ctx.enter_context(nc.Block())

        STEPS = GROUPS + 2
        PEELED = 4

        def run_part1(eng, step):
            for s in range(PEELED):
                step(Turn(0, 2, s), s)
            loops = (GROUPS - 2 - PEELED) // 2
            with eng.Fori(0, loops) as i:
                for c in range(2):
                    step(Turn(i, 2, PEELED + c), None)
            for s in range(PEELED + 2 * loops, STEPS):
                step(Turn(0, 2, s), s)

        def stages(s):
            if s is None:
                return True, True, True, True
            return s < GROUPS, 1 <= s <= GROUPS, 2 <= s, s + 1 < GROUPS

        STEPS2 = SLOTS + 4
        PEELED2 = 8

        def run_part2(eng, step):
            for s in range(PEELED2):
                step(Turn(0, 4, s), s)
            loops = (SLOTS - PEELED2) // 4
            with eng.Fori(0, loops) as i:
                for c in range(4):
                    step(Turn(i, 4, PEELED2 + c), None)
            for s in range(PEELED2 + 4 * loops, STEPS2):
                step(Turn(0, 4, s), s)

        def in_slots(s, back):
            return s is None or back <= s < SLOTS + back

        @block.sync
        def _(sp):
            sp.dma_start(tokw_raw[:, :], tok_w.rearrange("d c k -> d (c k)")).then_inc(weights_in, 16)
            for g in range(2):
                sp.dma_start(x_in[:, g], x_rows[g * PER * TX:(g + 1) * PER * TX, :]
                             .rearrange("(j p) c -> p j c", p=128)).then_inc(x_loaded[g], 16)
            for dst, src in ((wq_s, wq), (wk_s, wk), (wv_s, wv), (wg_s, wg)):
                sp.dma_start(dst[:, :], src).then_inc(weights_in, 16)
            for dst, src in ((bq_s, bq), (bk_s, bk)):
                sp.dma_start(dst[:, :], src.rearrange("(p a) -> p a", a=1)).then_inc(weights_in, 16)
            sp.dma_start(bv_s[:, :], bv.rearrange("(a n) -> a n", a=1).to_broadcast((128, D))).then_inc(weights_in, 16)
            sp.dma_start(bg_s[:, :], bg.rearrange("(a n) -> a n", a=1).to_broadcast((128, E))).then_inc(weights_in, 16)
            sp.dma_start(w1_s[:, :, :], w1.rearrange("e d h -> d e h")).then_inc(late_in, 16)
            for n in range(HC):
                sp.dma_start(w2_s[:, :, n, :], w2[:, n * 128:(n + 1) * 128, :].rearrange("e p d -> p e d"))\
                  .then_inc(late_in, 16)
            sp.dma_start(b1_s[:, :, :].rearrange("p e h -> p (e h)"),
                         b1.rearrange("(a e) h -> a (e h)", a=1).to_broadcast((128, E * H))).then_inc(late_in, 16)
            sp.dma_start(b2_s[:, :, 0:D], b2.unsqueeze(0).to_broadcast((128, E, D))).then_inc(late_in, 16)
            sp.wait_ge(padding_made, 3)
            sp.dma_start(routed[PADDING:PADDING + 128, :], padding_rows[:, :]).then_inc(padding_out, 16)

            def load_x(g):
                sp.wait_ge(x_turned, g.count(1, -1))
                sp.dma_start(x_in[:, g.slot], x_rows[bass.ds(g.count(PER * TX), PER * TX), :]
                             .rearrange("(j p) c -> p j c", p=128)).then_inc(x_loaded[g.slot], 16)

            with sp.Fori(1, GROUPS // 2) as i:
                for c in range(2):
                    load_x(Turn(i, 2, c))

            sp.wait_ge(ends_ready, 1)
            for e in range(E):
                end = sp.value_load(row_end[0:1, e:e + 1], min_val=e * REGION, max_val=e * REGION + N)
                sp.dma_start(routed[bass.ds(end, 128), :], padding_rows[:, :]).then_inc(padding_out, 16)

            sp.wait_ge(table_ready, 1)
            sp.wait_ge(padding_out, 16 * (E + 1))
            for n in range(2):
                sp.wait_ge(routed_out[n], 16 * TILES * GROUPS // 2)

            def load_slot(j):
                if j.at_least(4):
                    sp.wait_ge(xs_ready, j.count(1, -3))
                    sp.wait_ge(res_ready, j.count(1, -3))
                at = sp.value_load(table[0:1, 0, bass.ds(j.count(1), 1)], min_val=0, max_val=PADDING)
                sp.dma_start(tl[:, j.slot], routed[bass.ds(at, 128), :]).then_inc(slot_loaded[j.slot], 16)

            for j in range(4):
                load_slot(Turn(0, 4, j))
            with sp.Fori(1, SLOTS // 4) as i:
                for c in range(4):
                    load_slot(Turn(i, 4, c))
            for j in range(SLOTS // 4 * 4, SLOTS):
                load_slot(Turn(0, 4, j))

        @block.gpsimd
        def _(pool):
            pool.memset(ident[:, :], 0.0).then_inc(const_steps, 1)
            pool.memset(mask_bf[:, :], 0.0).then_inc(const_steps, 1)
            pool.memset(before_bf[:, :], 1.0).then_inc(const_steps, 1)
            pool.memset(padding_rows[:, 0:TOKEN], 0.0).then_inc(padding_made, 1)
            pool.memset(padding_rows[:, TOKEN:ROW], NOWHERE).then_inc(padding_made, 1)
            pool.memset(b2_s[:, :, D:ROW], 0.0).then_inc(padding_made, 1)
            pool.memset(ones_bf[:, :], 1.0).then_inc(consts_made, 1)
            pool.memset(eps_s[:, :], EPS).then_inc(consts_made, 1)
            pool.memset(power_s[:, :], -0.5).then_inc(consts_made, 1)
            pool.memset(zero_s[:, :], 0.0).then_inc(consts_made, 1)
            pool.memset(group_step[:, :], float(GT)).then_inc(consts_made, 1)
            pool.memset(ones_e[:, :], 1.0).then_inc(consts_made, 1)
            pool.iota(ramp[:, :], [[-1, E]], base=E, channel_multiplier=0,
                      allow_small_or_imprecise_dtypes=True).then_inc(consts_made, 1)
            pool.iota(next_token[:, :], [[HALF, TILES]], base=0, channel_multiplier=1,
                      allow_small_or_imprecise_dtypes=True).then_inc(consts_made, 1)
            pool.iota(base[:, :], [[REGION, E]], base=0, channel_multiplier=0,
                      allow_small_or_imprecise_dtypes=True).then_inc(consts_made, 1)
            pool.iota(region_at[:, :], [[REGION, E]], base=0, channel_multiplier=0,
                      allow_small_or_imprecise_dtypes=True).then_inc(consts_made, 1)
            pool.iota(slot_no[:, :, :], [[1, SLOTS], [0, E]], base=0, channel_multiplier=0,
                      allow_small_or_imprecise_dtypes=True).then_inc(consts_made, 1)
            pool.iota(slot_row[:, :, :], [[128, SLOTS], [0, E]], base=-PADDING, channel_multiplier=0,
                      allow_small_or_imprecise_dtypes=True).then_inc(consts_made, 1)
            pool.wait_ge(const_steps, 3)
            pool.affine_select(out=ident[:, :], in_=ident[:, :], compare_op=ALU.not_equal, fill=1.0, base=0,
                               pattern=[[-1, 128]], channel_multiplier=1).then_inc(consts_made, 1)
            pool.affine_select(out=mask_bf[:, :], in_=mask_bf[:, :], compare_op=ALU.is_ge, fill=MASKED, base=0,
                               pattern=[[1, HALF]], channel_multiplier=-1).then_inc(consts_made, 1)
            pool.affine_select(out=before_bf[:, :], in_=before_bf[:, :], compare_op=ALU.is_gt, fill=0.0, base=0,
                               pattern=[[1, HALF]], channel_multiplier=-1).then_inc(consts_made, 1)
            pool.wait_ge(consts_made, 15)

            def rstd(var, moments_ready, var_ready, rstd_ready, g):
                pool.wait_ge(moments_ready, g.count(1, 1))
                pool.tensor_tensor(var, var, eps_s[0:HALF, :], ALU.add).then_inc(var_ready, 1)
                pool.wait_ge(var_ready, g.count(1, 1))
                pool.tensor_tensor(var, var, power_s[0:HALF, :], ALU.pow).then_inc(rstd_ready, 1)

            def step(t, s):
                A, B_, C, _ = stages(s)
                g, a, r = t, t + -1, t + -2
                if C:
                    rstd(rows[0:HALF, r.slot, :, RSTD], moments2_ready, var2_ready, rstd2_ready, r)
                if B_:
                    rstd(moments1[0:HALF, :, 1], moments1_ready, var1_ready, rstd1_ready, a)
                if A:
                    for k in range(1, 4):
                        pool.wait_ge(conv_mul, g.count(TAPS, k + 1))
                        if k > 1:
                            pool.wait_ge(pool_sum, g.count(3, k - 1))
                        pool.tensor_tensor(prod[:, 0], prod[:, 0], prod[:, k], ALU.add).then_inc(pool_sum, 1)
                if C:
                    if r.at_least(1):
                        pool.wait_ge(token_next, r.count(1))
                    pool.wait_ge(place_ready, r.count(1, 1))
                    pool.tensor_tensor(rows[0:HALF, r.slot, :, TOKEN], next_token[0:HALF, :], zero_s[0:HALF, :],
                                       ALU.add).then_inc(token_written, 1)
                    pool.wait_ge(token_written, r.count(1, 1))
                    pool.tensor_tensor(next_token[:, :], next_token[:, :], group_step[:, :], ALU.add)\
                        .then_inc(token_next, 1)
                    for j in range(TILES):
                        pool.indirect_dma_start(
                            out=routed, out_offset=bass.IndirectOffsetOnAxis(ap=row_at[0:HALF, r.slot, j:j + 1], axis=0),
                            in_=rows[0:HALF, r.slot, j, :], in_offset=None).then_inc(routed_out[r.slot], 16)

            run_part1(pool, step)

            pool.wait_ge(table_ready, 1)
            pool.wait_ge(late_in, 16 * (3 + HC))

            def step2(t, s):
                if in_slots(s, 0):
                    j = t
                    e = pool.value_load(table[0:1, 1, bass.ds(j.count(1), 1)], min_val=0, max_val=E - 1)
                    pool.wait_ge(slot_loaded[j.slot], j.rounds(16, 16))
                    if j.at_least(4):
                        pool.wait_ge(done_ready, j.count(1, -3))
                    pool.tensor_tensor(res[:, j.slot], tl[:, j.slot],
                                       b2_s[:, bass.ds(e, 1), :].rearrange("p a d -> p (a d)"), ALU.add)\
                        .then_inc(res_ready, 1)
                if in_slots(s, 4):
                    j = t + -4
                    if not in_slots(s, 0):
                        pool.wait_ge(done_ready, j.count(1, 1))
                    pool.indirect_dma_start(
                        out=out_rows, out_offset=bass.IndirectOffsetOnAxis(ap=token_at[:, j.slot:j.slot + 1], axis=0),
                        in_=done_rows[:, j.slot], in_offset=None,
                        bounds_check=N - 1, oob_is_err=False).then_inc(done_out[j.slot], 16)

            run_part2(pool, step2)
            for n in range(4):
                pool.wait_ge(done_out[n], 16 * len(range(n, SLOTS, 4)))

        @block.scalar
        def _(act):
            for n in range(2):
                act.wait_ge(tokw_turned, n + 1)
                src = conv_bank[n][:, :].rearrange("p (k d) -> p k d", d=D)
                take = min(4, TAPS - 4 * n)
                act.activation(tokw[:, 4 * n:4 * n + take, :], src[:, 0:take, :], ACT.Copy).then_inc(tokw_ready, 1)

            def xT_copy(g):
                act.wait_ge(x_turned, g.count(1, 1))
                if g.at_least(2):
                    act.wait_ge(conv_mul, g.count(TAPS, -TAPS))
                act.activation(xT[:, g.slot].rearrange("p b t -> p (b t)"), turn_bank[:, :], ACT.Copy)\
                    .then_inc(xT_ready, 1)

            def tanh(g, k):
                act.wait_ge(conv_mm, g.count(TAPS, k + 1))
                bank = conv_bank[(k + g.slot) % BANKS][:, 0:GT]
                act.activation(bank, bank, ACT.Tanh).then_inc(conv_tanh, 1)

            act.wait_ge(weights_in, 16 * 9)
            xT_copy(Turn(0, 2, 0))

            def step(t, s):
                A, B_, C, NEXT = stages(s)
                g, a, r = t, t + -1, t + -2
                if A:
                    tanh(g, 0)
                    tanh(g, 1)
                if C:
                    act.wait_ge(xf_turned, r.count(1, 1))
                    act.wait_ge(gate_mm, r.count(1))
                    act.activation(xfT[:, :, :].rearrange("p j t -> p (j t)"), turn_bank[:, 0:GT], ACT.Copy)\
                        .then_inc(xfT_ready, 1)
                if A:
                    tanh(g, 2)
                if B_:
                    act.wait_ge(m_turned, a.count(1, 1))
                    act.wait_ge(v_mm, a.count(1))
                    act.activation(mT[:, :, :].rearrange("p j t -> p (j t)"), k_bank[:, 0:GT], ACT.Copy)\
                        .then_inc(mT_ready, 1)
                if A:
                    tanh(g, 3)
                if B_:
                    act.wait_ge(q_mm, a.count(1, 1))
                    act.wait_ge(scores_mm, a.count(PER))
                    act.activation(qT[:, :, :].rearrange("p b t -> p (b t)"), q_bank[:, 0:GT], ACT.Identity,
                                   bias=bq_s[:, 0:1]).then_inc(q_ready, 1)
                    act.wait_ge(k_mm, a.count(1, 1))
                    act.activation(kT[:, :, :].rearrange("p b t -> p (b t)"), k_bank[:, 0:GT], ACT.Identity,
                                   bias=bk_s[:, 0:1]).then_inc(k_ready, 1)
                if A:
                    tanh(g, 4)
                if B_:
                    for b in range(PER):
                        act.wait_ge(max_ready, a.count(PER, b + 1))
                        act.wait_ge(read_mm, a.count(1))
                        for c, (lo, hi) in enumerate(((0, L), (L, L + HALF))):
                            n = 2 * b + c
                            ins = act.activation(probs[0:HALF, b, lo:hi], score_bank[b][0:HALF, lo:hi], ACT.Exp,
                                                 bias=neg_max[0:HALF, n:n + 1], accum_out=den[0:HALF, n:n + 1])
                        ins.then_inc(probs_ready, 1)
                if A:
                    tanh(g, 5)
                    tanh(g, 6)
                if NEXT:
                    xT_copy(t + 1)

            run_part1(act, step)

            def step2(t, s):
                if in_slots(s, 0):
                    j = t
                    act.wait_ge(xs_turned, j.count(1, 1))
                    if j.at_least(2):
                        act.wait_ge(layer1_mm, j.count(1, -1))
                    act.activation(xsT[:, j.slot % 2], conv_bank[j.slot % 2][:, 0:128], ACT.Copy)\
                        .then_inc(xsT_ready, 1)
                if in_slots(s, 2):
                    j = t + -2
                    act.wait_ge(hid_turned, j.count(1, 1))
                    if j.at_least(2):
                        act.wait_ge(layer2_mm, j.count(1, -1))
                    act.activation(hidT[:, j.slot % 2], hidT_bank[j.slot % 2][:, 0:H], ACT.Relu)\
                        .then_inc(hidT_ready, 1)

            run_part2(act, step2)

        @block.vector
        def _(dve):
            def normalize(dst, src, mean, rstd):
                return dve.tensor_scalar(dst, src, mean, rstd, ALU.subtract, ALU.mult)

            dve.wait_ge(consts_made, 15)
            dve.wait_ge(weights_in, 16 * 9)
            dve.tensor_copy(ident_bf[:, :], ident[:, :]).then_inc(consts_made, 1)

            def mul(g, k):
                dve.wait_ge(conv_tanh, g.count(TAPS, k + 1))
                if k == 0 and g.at_least(1):
                    dve.wait_ge(pool_sum, g.count(3))
                w = conv_bank[(k + g.slot) % BANKS][:, 0:GT].rearrange("p (b t) -> p b t", b=PER)
                dve.tensor_tensor(prod[:, k].rearrange("p (b t) -> p b t", b=PER), w, xT[:, g.slot, :, k:k + L],
                                  ALU.mult).then_inc(conv_mul, 1)

            def step(t, s):
                A, B_, C, _ = stages(s)
                g, a, r = t, t + -1, t + -2
                h = tiles_of(h_bank)
                rr = rows[0:HALF, r.slot]
                if C:
                    dve.wait_ge(h2_ready, r.count(1, 1))
                    for j in range(TILES):
                        ins = dve.bn_stats(stats2[0:HALF, j, :], rr[:, j, 0:D])
                    ins.then_inc(stats2_ready, 1)
                    dve.wait_ge(stats2_ready, r.count(1, 1))
                if B_:
                    dve.wait_ge(h_turned, a.count(1, 1))
                    for j in range(TILES):
                        ins = dve.bn_stats(stats1[0:HALF, j, :], h[:, j, :])
                    ins.then_inc(stats1_ready, 1)
                if C:
                    for j in range(TILES):
                        ins = dve.bn_aggr(rr[:, j, MEAN:MEAN + 2], stats2[0:HALF, j, :])
                    ins.then_inc(moments2_ready, 1)
                if B_:
                    dve.wait_ge(stats1_ready, a.count(1, 1))
                if A:
                    mul(g, 0)
                if B_:
                    for j in range(TILES):
                        ins = dve.bn_aggr(moments1[0:HALF, j, :], stats1[0:HALF, j, :])
                    ins.then_inc(moments1_ready, 1)
                if A:
                    mul(g, 1)
                if C:
                    dve.wait_ge(rstd2_ready, r.count(1, 1))
                    if r.at_least(1):
                        dve.wait_ge(xf_turned, r.count(1))
                    for j in range(TILES):
                        ins = normalize(xf[0:HALF, j, :], rr[:, j, 0:D], rr[:, j, MEAN:MEAN + 1], rr[:, j, RSTD:RSTD + 1])
                    ins.then_inc(xf_ready, 1)
                if B_:
                    dve.wait_ge(rstd1_ready, a.count(1, 1))
                    for j in range(TILES):
                        ins = normalize(m[0:HALF, j, :], h[:, j, :], moments1[0:HALF, j, 0:1], moments1[0:HALF, j, 1:2])
                    ins.then_inc(m_ready, 1)
                    dve.wait_ge(m_ready, a.count(1, 1))
                    dve.tensor_tensor(hm[0:HALF], h, m[0:HALF], ALU.add).then_inc(hm_ready, 1)
                if A:
                    mul(g, 2)
                    mul(g, 3)
                if C:
                    dve.wait_ge(gate_mm, r.count(1, 1))
                    dve.tensor_tensor(logits[0:HALF], gate_out, bg_s[0:HALF].unsqueeze(1).to_broadcast((HALF, TILES, E)),
                                      ALU.add).then_inc(choice_steps, 1)
                    dve.wait_ge(choice_steps, r.count(5, 1))
                    dve.tensor_reduce(top[0:HALF], logits[0:HALF], axis=AX.X, op=ALU.max).then_inc(choice_steps, 1)
                    dve.wait_ge(choice_steps, r.count(5, 2))
                    dve.tensor_tensor(is_top[0:HALF], logits[0:HALF],
                                      top[0:HALF].unsqueeze(2).to_broadcast((HALF, TILES, E)), ALU.is_equal)\
                        .then_inc(choice_steps, 1)
                    dve.wait_ge(choice_steps, r.count(5, 3))
                    dve.tensor_tensor(top_ramp[0:HALF], is_top[0:HALF],
                                      ramp[0:HALF].unsqueeze(1).to_broadcast((HALF, TILES, E)), ALU.mult)\
                        .then_inc(choice_steps, 1)
                    dve.wait_ge(choice_steps, r.count(5, 4))
                    dve.tensor_reduce(first[0:HALF], top_ramp[0:HALF], axis=AX.X, op=ALU.max).then_inc(choice_steps, 1)
                    dve.wait_ge(choice_steps, r.count(5, 5))
                    dve.tensor_tensor(onehot[0:HALF], ramp[0:HALF].unsqueeze(1).to_broadcast((HALF, TILES, E)),
                                      first[0:HALF].unsqueeze(2).to_broadcast((HALF, TILES, E)), ALU.is_equal)\
                        .then_inc(onehot_ready, 1)
                if A:
                    mul(g, 4)
                if B_:
                    dve.wait_ge(v_mm, a.count(1, 1))
                    dve.tensor_tensor(vb[0:HALF], tiles_of(turn_bank),
                                      bv_s[0:HALF].unsqueeze(1).to_broadcast((HALF, TILES, D)), ALU.add)\
                        .then_inc(v_ready, 1)
                    for b in range(PER):
                        dve.wait_ge(scores_mm, a.count(PER, b + 1))
                        for c, (lo, hi) in enumerate(((0, L), (L, L + HALF))):
                            ins = dve.tensor_reduce(neg_max[0:HALF, 2 * b + c:2 * b + c + 1],
                                                    score_bank[b][0:HALF, lo:hi], axis=AX.X, op=ALU.max, negate=True)
                        ins.then_inc(max_ready, 1)
                if A:
                    mul(g, 5)
                if C:
                    dve.wait_ge(rank_mm, r.count(1, 1))
                    if r.at_least(1):
                        dve.wait_ge(base_ready, r.count(1))
                    dve.tensor_tensor(place[0:HALF], rank_out, base[0:HALF].unsqueeze(1).to_broadcast((HALF, TILES, E)),
                                      ALU.add).then_inc(place_steps, 1)
                    dve.wait_ge(place_steps, r.count(3, 1))
                    dve.tensor_tensor(base[0:HALF], base[0:HALF], total_out, ALU.add).then_inc(base_ready, 1)
                    dve.tensor_tensor(place1[0:HALF], place[0:HALF], onehot[0:HALF], ALU.mult).then_inc(place_steps, 1)
                    dve.wait_ge(place_steps, r.count(3, 2))
                    dve.tensor_reduce(row_sum[0:HALF], place1[0:HALF], axis=AX.X, op=ALU.add).then_inc(place_steps, 1)
                    dve.wait_ge(place_steps, r.count(3, 3))
                    if r.at_least(2):
                        dve.wait_ge(routed_out[r.slot], r.rounds(16 * TILES))
                    dve.tensor_copy(row_at[0:HALF, r.slot], row_sum[0:HALF]).then_inc(place_ready, 1)
                if B_:
                    dve.wait_ge(probs_ready, a.count(PER, PER))
                    dve.reciprocal(rden[0:HALF], den[0:HALF]).then_inc(rden_ready, 1)
                    dve.wait_ge(rden_ready, a.count(1, 1))
                    if a.at_least(1):
                        dve.wait_ge(read_mm, a.count(1))
                    for j in range(TILES):
                        ins = dve.tensor_scalar(vs[0:HALF, j, :], vb[0:HALF, j, :], rden[0:HALF, j:j + 1], READ_SCALE,
                                                ALU.mult, ALU.mult)
                    ins.then_inc(vs_ready, 1)
                if A:
                    mul(g, 6)
                    dve.wait_ge(conv_mul, g.count(TAPS, 6))
                    dve.tensor_tensor(prod[:, 4], prod[:, 4], prod[:, 5], ALU.add).then_inc(vector_sum, 1)
                    dve.wait_ge(vector_sum, g.count(2, 1))
                    dve.tensor_tensor(prod[:, 4], prod[:, 4], prod[:, 6], ALU.add).then_inc(vector_sum, 1)
                    dve.wait_ge(vector_sum, g.count(2, 2))
                    dve.wait_ge(pool_sum, g.count(3, 3))
                    if g.at_least(1):
                        dve.wait_ge(h_turned, g.count(1))
                    dve.tensor_tensor(hT[:, :, :].rearrange("p j t -> p (j t)"), prod[:, 0], prod[:, 4], ALU.add)\
                        .then_inc(h_ready, 1)
                if B_:
                    dve.wait_ge(read_mm, a.count(1, 1))
                    if a.at_least(2):
                        dve.wait_ge(routed_out[a.slot], a.rounds(16 * TILES))
                    dve.tensor_tensor(rows[0:HALF, a.slot, :, 0:D], tiles_of(h_bank), hm[0:HALF], ALU.add)\
                        .then_inc(h2_ready, 1)

            run_part1(dve, step)

            done = [0]

            def then(ins):
                done[0] += 1
                ins.then_inc(table_steps, 1)
                dve.wait_ge(table_steps, done[0])

            dve.wait_ge(base_ready, GROUPS)
            dve.tensor_copy(row_end[:, :], base[0:1, :]).then_inc(ends_ready, 1)
            then(dve.tensor_tensor(held[:, :], base[0:1, :], region_at[:, :], ALU.subtract))
            then(dve.tensor_scalar(held_up[:, :], held[:, :], 127.0, None, ALU.add))
            then(dve.tensor_single_scalar(tiles_i[:, :], held_up[:, :], 7, ALU.arith_shift_right))
            then(dve.tensor_copy(tiles_f[:, :], tiles_i[:, :]))
            then(dve.tensor_tensor_scan(tile_end[:, :], ones_e[:, :], tiles_f[:, :], 0.0, ALU.mult, ALU.add))
            then(dve.tensor_tensor(tile_start[:, :], tile_end[:, :], tiles_f[:, :], ALU.subtract))
            then(dve.scalar_tensor_tensor(shift_e[:, :], tile_start[:, :], -128.0, region_at[:, :], ALU.mult, ALU.add))

            def over_slots(t):
                return t[:, :].unsqueeze(1).to_broadcast((1, SLOTS, E))

            then(dve.tensor_tensor(begun[:, :, :], slot_no[:, :, :], over_slots(tile_start), ALU.is_ge))
            then(dve.tensor_tensor(ended[:, :, :], slot_no[:, :, :], over_slots(tile_end), ALU.is_ge))
            then(dve.tensor_tensor(begun[:, :, :], begun[:, :, :], ended[:, :, :], ALU.subtract))
            then(dve.tensor_tensor(at_e[:, :, :], slot_row[:, :, :], over_slots(shift_e), ALU.add))
            then(dve.tensor_tensor(at_e[:, :, :], at_e[:, :, :], begun[:, :, :], ALU.mult))
            then(dve.tensor_reduce(table_f[:, 0, :], at_e[:, :, :], axis=AX.X, op=ALU.add))
            then(dve.tensor_reduce(table_f[:, 1, :], ended[:, :, :], axis=AX.X, op=ALU.add))
            then(dve.tensor_scalar(table[:, 0, :], table_f[:, 0, :], float(PADDING), None, ALU.add))
            dve.tensor_scalar(table[:, 1, :], table_f[:, 1, :], float(E - 1), None, ALU.min).then_inc(table_ready, 1)
            dve.wait_ge(table_ready, 1)

            dve.wait_ge(late_in, 16 * (3 + HC))

            def step2(t, s):
                if in_slots(s, 0):
                    j = t
                    dve.wait_ge(slot_loaded[j.slot], j.rounds(16, 16))
                    if j.at_least(2):
                        dve.wait_ge(xs_turned, j.count(1, -1))
                    normalize(xs[:, j.slot % 2], tl[:, j.slot, 0:D], tl[:, j.slot, MEAN:MEAN + 1],
                              tl[:, j.slot, RSTD:RSTD + 1]).then_inc(xs_ready, 1)
                if in_slots(s, 1):
                    j = t + -1
                    e = dve.value_load(table[0:1, 1, bass.ds(j.count(1), 1)], min_val=0, max_val=E - 1)
                    dve.wait_ge(layer1_mm, j.count(1, 1))
                    if j.at_least(2):
                        dve.wait_ge(hid_turned, j.count(1, -1))
                    dve.tensor_tensor(hid[:, j.slot % 2], hid_bank[j.slot % 2][:, 0:H],
                                      b1_s[:, bass.ds(e, 1), :].rearrange("p a h -> p (a h)"), ALU.add)\
                        .then_inc(hid_ready, 1)
                if in_slots(s, 4):
                    j = t + -4
                    dve.wait_ge(layer2_mm, j.count(1, 1))
                    dve.wait_ge(res_ready, j.count(1, 1))
                    if j.at_least(4):
                        dve.wait_ge(done_out[j.slot], j.rounds(16))
                    dve.tensor_copy(token_at[:, j.slot:j.slot + 1], res[:, j.slot, TOKEN:TOKEN + 1])
                    dve.tensor_tensor(done_rows[:, j.slot], y_bank[j.slot % 2][:, 0:D], res[:, j.slot, 0:D], ALU.add)\
                        .then_inc(done_ready, 1)

            run_part2(dve, step2)

        @block.tensor
        def _(pe):
            pe.wait_ge(weights_in, 16 * 9)
            pe.wait_ge(consts_made, 16)
            raw = tokw_raw[:, :].rearrange("d (c k) -> d k c", k=TAPS)
            for k in range(TAPS):
                ins = pe.transpose(conv_bank[k // 4][:, k % 4 * 128:(k % 4 + 1) * 128], raw[:, k, :], ident[:, :])
                if k == 3 or k == TAPS - 1:
                    ins.then_inc(tokw_turned, 1)

            def turn_x(g):
                pe.wait_ge(x_loaded[g.slot], g.rounds(16, 16))
                if g.at_least(2):
                    pe.wait_ge(v_ready, g.count(1, -1))
                elif g.at_least(1):
                    pe.wait_ge(xT_ready, 1)
                for j in range(4):
                    ins = pe.transpose(turn_bank[:, j * 128:(j + 1) * 128], x_in[:, g.slot, j, :], ident[:, :])
                ins.then_inc(x_turned, 1)

            turn_x(Turn(0, 2, 0))
            pe.wait_ge(tokw_ready, 2)

            def conv(g, k):
                if k == 0:
                    pe.wait_ge(xT_ready, g.count(1, 1))
                n = (k + g.slot) % BANKS
                if k >= BANKS:
                    pe.wait_ge(conv_mul, g.count(TAPS, k - BANKS + 1))
                elif g.at_least(1):
                    last = max(q for q in range(TAPS) if (q + 1 - g.slot) % BANKS == n)
                    pe.wait_ge(conv_mul, g.count(TAPS, last + 1 - TAPS))
                pe.matmul(conv_bank[n][:, 0:GT], tokw[:, k, :], xT[:, g.slot, :, TAPS - 1:TX],
                          start=True, stop=True).then_inc(conv_mm, 1)

            def step(t, s):
                A, B_, C, NEXT = stages(s)
                g, a, r = t, t + -1, t + -2
                if B_:
                    pe.wait_ge(h_ready, a.count(1, 1))
                    if a.at_least(1):
                        pe.wait_ge(h2_ready, a.count(1))
                    for j in range(TILES):
                        ins = pe.transpose(tiles_of(h_bank)[:, j, :], hT[:, j, :], ident[:, :])
                    ins.then_inc(h_turned, 1)
                if A:
                    conv(g, 0)
                    conv(g, 1)
                if C:
                    pe.wait_ge(xf_ready, r.count(1, 1))
                    pe.wait_ge(xT_ready, r.count(1, 3) if s is None else min(s + 1, GROUPS))
                    if s is not None and s >= GROUPS:
                        pe.wait_ge(v_ready, min(s - 1, GROUPS))
                    for j in range(TILES):
                        ins = pe.transpose(turn_bank[:, j * HALF:(j + 1) * HALF], xf[0:HALF, j, :], ident[0:HALF, 0:HALF])
                    ins.then_inc(xf_turned, 1)
                if A:
                    conv(g, 2)
                    conv(g, 3)
                if B_:
                    pe.wait_ge(m_ready, a.count(1, 1))
                    if a.at_least(1):
                        pe.wait_ge(probs_ready, a.count(PER))
                    for j in range(TILES):
                        ins = pe.transpose(k_bank[:, j * HALF:(j + 1) * HALF], m[0:HALF, j, :], ident[0:HALF, 0:HALF])
                    ins.then_inc(m_turned, 1)
                if C:
                    pe.wait_ge(xfT_ready, r.count(1, 1))
                    if r.at_least(1):
                        pe.wait_ge(base_ready, r.count(1))
                    for j in range(TILES):
                        ins = pe.matmul(gate_out[:, j, :], xfT[:, j, :], wg_s[:, :], start=True, stop=True)
                    ins.then_inc(gate_mm, 1)
                if B_:
                    pe.wait_ge(mT_ready, a.count(1, 1))
                    every = mT[:, :, :].rearrange("p j t -> p (j t)")
                    pe.matmul(q_bank[:, 0:GT], wq_s[:, :], every, start=True, stop=True).then_inc(q_mm, 1)
                    pe.matmul(k_bank[:, 0:GT], wk_s[:, :], every, start=True, stop=True).then_inc(k_mm, 1)
                    if a.at_least(1):
                        pe.wait_ge(xfT_ready, a.count(1))
                    else:
                        pe.wait_ge(xT_ready, 2)
                    for j in range(TILES):
                        ins = pe.matmul(tiles_of(turn_bank)[:, j, :], mT[:, j, :], wv_s[:, :], start=True, stop=True)
                    ins.then_inc(v_mm, 1)
                if A:
                    conv(g, 4)
                if B_:
                    pe.wait_ge(q_ready, a.count(1, 1))
                    pe.wait_ge(k_ready, a.count(1, 1))
                    for b in range(PER):
                        for c, (lo, hi) in enumerate(((0, L), (L, L + HALF))):
                            pe.matmul(score_bank[b][0:HALF, lo:hi], kT[:, b, c * HALF:(c + 1) * HALF],
                                      qT[:, b, c * HALF:L], start=True, stop=False)
                            ins = pe.matmul(score_bank[b][0:HALF, lo:lo + HALF], ident_bf[0:HALF, 0:HALF],
                                            mask_bf[0:HALF, :], start=False, stop=True)
                        ins.then_inc(scores_mm, 1)
                if C:
                    pe.wait_ge(onehot_ready, r.count(1, 1))
                    pe.matmul(rank_out, before_bf[0:HALF, :], onehot[0:HALF], start=True, stop=False)
                    for j in range(TILES - 1):
                        n = TILES - 1 - j
                        pe.matmul(rank_out[:, j + 1:], ones_bf[0:HALF, 0:HALF],
                                  onehot[0:HALF, j:j + 1, :].to_broadcast((HALF, n, E)), start=False, stop=(n == 1))
                    for j in range(TILES):
                        ins = pe.matmul(total_out, ones_bf[0:HALF, 0:HALF], onehot[0:HALF, j, :],
                                        start=(j == 0), stop=(j == TILES - 1))
                    ins.then_inc(rank_mm, 1)
                if A:
                    conv(g, 5)
                    conv(g, 6)
                if B_:
                    pe.wait_ge(vs_ready, a.count(1, 1))
                    pe.wait_ge(hm_ready, a.count(1, 1))
                    read = tiles_of(h_bank)
                    for b in range(PER):
                        pe.matmul(read[:, 2 * b, :], probs[0:HALF, b, 0:HALF], vs[0:HALF, 2 * b, :],
                                  start=True, stop=True)
                        pe.matmul(read[:, 2 * b + 1, :], probs[0:HALF, b, HALF:L], vs[0:HALF, 2 * b, :],
                                  start=True, stop=False)
                        ins = pe.matmul(read[:, 2 * b + 1, :], probs[0:HALF, b, L:L + HALF], vs[0:HALF, 2 * b + 1, :],
                                        start=False, stop=True)
                    ins.then_inc(read_mm, 1)
                if NEXT:
                    turn_x(t + 1)

            run_part1(pe, step)

            pe.wait_ge(table_ready, 1)
            pe.wait_ge(late_in, 16 * (3 + HC))

            def expert(j):
                return pe.value_load(table[0:1, 1, bass.ds(j.count(1), 1)], min_val=0, max_val=E - 1)

            def step2(t, s):
                if in_slots(s, 1):
                    j = t + -1
                    e = expert(j)
                    pe.wait_ge(xsT_ready, j.count(1, 1))
                    if j.at_least(2):
                        pe.wait_ge(hid_ready, j.count(1, -1))
                    pe.matmul(hid_bank[j.slot % 2][:, 0:H], xsT[:, j.slot % 2],
                              w1_s[:, bass.ds(e, 1), :].rearrange("p a h -> p (a h)"), start=True, stop=True)\
                        .then_inc(layer1_mm, 1)
                if in_slots(s, 2):
                    j = t + -2
                    pe.wait_ge(hid_ready, j.count(1, 1))
                    if j.at_least(2):
                        pe.wait_ge(hidT_ready, j.count(1, -1))
                    for n in range(HC):
                        ins = pe.transpose(hidT_bank[j.slot % 2][:, n * 128:(n + 1) * 128],
                                           hid[:, j.slot % 2, n * 128:(n + 1) * 128], ident[:, :])
                    ins.then_inc(hid_turned, 1)
                if in_slots(s, 3):
                    j = t + -3
                    e = expert(j)
                    pe.wait_ge(hidT_ready, j.count(1, 1))
                    if j.at_least(2):
                        pe.wait_ge(done_ready, j.count(1, -1))
                    for n in range(HC):
                        ins = pe.matmul(y_bank[j.slot % 2][:, 0:D], hidT[:, j.slot % 2, n * 128:(n + 1) * 128],
                                        w2_s[:, bass.ds(e, 1), n, :].rearrange("p a d -> p (a d)"),
                                        start=(n == 0), stop=(n == HC - 1))
                    ins.then_inc(layer2_mm, 1)
                if in_slots(s, 0):
                    j = t
                    pe.wait_ge(xs_ready, j.count(1, 1))
                    if j.at_least(2):
                        pe.wait_ge(xsT_ready, j.count(1, -1))
                    pe.transpose(conv_bank[j.slot % 2][:, 0:128], xs[:, j.slot % 2], ident[:, :]).then_inc(xs_turned, 1)

            run_part2(pe, step2)


_INS = ['x', 'L0_tok_weights', 'L0_attn_Wk', 'L0_attn_bk', 'L0_attn_Wq', 'L0_attn_bq', 'L0_attn_Wv', 'L0_attn_bv',
        'L0_ffn_W1', 'L0_ffn_b1', 'L0_ffn_W2', 'L0_ffn_b2', 'L0_ffn_Wg', 'L0_ffn_bg']


def kernel(**inputs):
    import numpy as _np
    import concourse.bacc as _bacc
    from concourse import mybir as _mybir
    from concourse.bass_utils import run_bass_kernel_spmd as _run

    nc = _bacc.Bacc("TRN2", target_bir_lowering=False, num_devices=1)
    arrays, args = {}, []
    for name in _INS:
        a = _np.ascontiguousarray(inputs[name])
        arrays[f"in_{name}_dram"] = a
        args.append(nc.dram_tensor(f"in_{name}_dram", a.shape, _mybir.dt.from_np(a.dtype), kind="ExternalInput").ap())
    b, t, c = inputs['x'].shape
    taps = inputs['L0_tok_weights'].shape[2]
    args.append(nc.dram_tensor("out_0_dram", (b, t - taps + 1, c), _mybir.dt.float32, kind="ExternalOutput").ap())
    audio_tower(nc, *args)
    r = _run(nc, [arrays], core_ids=[0])
    return r.results[0]["out_0_dram"]
```

```python
from contextlib import ExitStack

import concourse.bass as bass
from concourse import mybir

FP32 = mybir.dt.float32
BF16 = mybir.dt.bfloat16
INT32 = mybir.dt.int32
UINT32 = mybir.dt.uint32
ALU = mybir.AluOpType
ACT = mybir.ActivationFunctionType
AX = mybir.AxisListType

MASKED = -1.0e30
EPS = 1e-5


class Turn:

    def __init__(self, loop, times, offset):
        self.loop, self.times, self.offset = loop, times, offset

    def __add__(self, n):
        return Turn(self.loop, self.times, self.offset + n)

    def of(self, n):
        return self.offset % n

    def count(self, per, extra=0):
        return self.loop * (self.times * per) + (self.offset * per + extra)

    def uses(self, n, per, extra=0):
        return self.loop * (self.times // n * per) + (self.offset // n * per + extra)

    def at_least(self, n):
        return not isinstance(self.loop, int) or self.offset >= n


def audio_tower(nc, x, tok_w, wk, bk, wq, bq, wv, bv, w1, b1, w2, b2, wg, bg, out):
    B, TX, D = x.shape
    TAPS = tok_w.shape[2]
    L = TX - TAPS + 1
    E, _, H = w1.shape
    N = B * L
    PER = 2
    GROUPS = B // PER
    HALF = L // 2
    TILES = 2 * PER
    GT = PER * L
    HC = H // 128
    REGION = -(-N // 128) * 128 + 128
    PADDING = E * REGION
    ROW = D + 3
    SHIFT, RSTD, TOKEN = D, D + 1, D + 2
    SLOTS = (N + E * 127) // 128
    TABLE = -(-SLOTS // 8) * 8
    NOWHERE = 1 << 20
    READ_SCALE = float(D) ** -0.5
    BANKS = 3
    RING = 8
    OUTS = 4

    x_rows = x.rearrange("b t c -> (b t) c")
    out_rows = out.rearrange("b t c -> (b t) c")
    routed = nc.dram_tensor("routed", (PADDING + 128, ROW), FP32).ap()

    ctx = ExitStack()
    with ctx:
        def sb(name, shape, dt=FP32):
            return ctx.enter_context(nc.sbuf_tensor(name, shape, dt))

        def pb(name):
            return ctx.enter_context(nc.psum_tensor(name, [128, 512], FP32))

        def sem(name):
            return ctx.enter_context(nc.semaphore(name))

        ident = sb("ident", [128, 128])
        ident_bf = sb("ident_bf", [128, 128], BF16)
        mask_bf = sb("mask_bf", [128, HALF], BF16)
        before_bf = sb("before_bf", [128, HALF], BF16)
        ones_bf = sb("ones_bf", [128, 128], BF16)
        tokw_raw = sb("tokw_raw", [128, D * TAPS])
        tokw = sb("tokw", [128, TAPS, D])
        wq_s = sb("wq_s", [128, D])
        wk_s = sb("wk_s", [128, D])
        wv_s = sb("wv_s", [128, D])
        bq_s = sb("bq_s", [128, 1])
        bk_s = sb("bk_s", [128, 1])
        bv_s = sb("bv_s", [128, D])
        wg_s = sb("wg_s", [128, E])
        bg_s = sb("bg_s", [128, E])
        w1_s = sb("w1_s", [128, E, H])
        w2_s = sb("w2_s", [128, E, HC, D])
        b1_s = sb("b1_s", [128, E, H])
        b2_s = sb("b2_s", [128, E, D])
        eps_s = sb("eps_s", [128, TILES])
        power_s = sb("power_s", [128, TILES])
        zero_s = sb("zero_s", [128, TILES])
        ramp = sb("ramp", [128, E])
        zero_u = sb("zero_u", [128, TILES], UINT32)
        next_token = sb("next_token", [128, TILES], UINT32)
        group_step = sb("group_step", [128, TILES], UINT32)
        base = sb("base", [128, E])
        padding_rows = sb("padding_rows", [128, ROW])

        x_in = sb("x_in", [128, 2, 4, 128])
        xT = sb("xT", [128, 2, PER, TX])
        prod = sb("prod", [128, 2, TAPS, GT])
        hT = sb("hT", [128, 2, TILES, HALF])
        stats1 = sb("stats1", [128, TILES, 6])
        norm1 = sb("norm1", [128, 2, TILES, 2])
        m = sb("m", [128, 2, TILES, 128])
        hm = sb("hm", [128, 2, TILES, 128])
        mT = sb("mT", [128, 2, TILES, HALF])
        qT = sb("qT", [128, 2, PER, L])
        kT = sb("kT", [128, 2, PER, L])
        vb = sb("vb", [128, 2, TILES, 128])
        vs = sb("vs", [128, 2, TILES, 128])
        neg_max = sb("neg_max", [128, 2, TILES])
        den = sb("den", [128, 2, TILES])
        rden = sb("rden", [128, 2, TILES])
        probs = sb("probs", [128, 2, PER, L + HALF])
        rows = sb("rows", [128, 2, TILES, ROW])
        stats2 = sb("stats2", [128, TILES, 6])
        xf = sb("xf", [128, 2, TILES, 128])
        xfT = sb("xfT", [128, 2, TILES, HALF])
        logits = sb("logits", [128, TILES, E])
        top = sb("top", [128, TILES])
        is_top = sb("is_top", [128, TILES, E])
        top_ramp = sb("top_ramp", [128, TILES, E])
        first = sb("first", [128, TILES])
        onehot = sb("onehot", [128, 2, TILES + 1, E], BF16)
        place = sb("place", [128, TILES, E])
        place1 = sb("place1", [128, TILES, E])
        row_sum = sb("row_sum", [128, TILES])
        row_at = sb("row_at", [128, 2, TILES], UINT32)

        region_up = sb("region_up", [TABLE, E])
        row_end = sb("row_end", [1, E], INT32)
        held_up = sb("held_up", [TABLE, E], INT32)
        tiles_i = sb("tiles_i", [TABLE, E], INT32)
        tiles_f = sb("tiles_f", [TABLE, E])
        ones_e = sb("ones_e", [TABLE, E])
        tile_end = sb("tile_end", [TABLE, E])
        skip = sb("skip", [TABLE, E])
        slot_no = sb("slot_no", [TABLE, E])
        ended = sb("ended", [TABLE, E])
        skipped = sb("skipped", [TABLE, E + 1])
        slot_at = sb("slot_at", [TABLE, 2])
        table = sb("table", [1, 2, TABLE], INT32)

        tl = sb("tl", [128, RING, ROW])
        xs = sb("xs", [128, 2, 128])
        xsT = sb("xsT", [128, 2, 128])
        hid = sb("hid", [128, 2, H])
        hidT = sb("hidT", [128, 2, H])
        res = sb("res", [128, RING, D])
        token_at = sb("token_at", [128, RING], UINT32)
        done_rows = sb("done_rows", [128, OUTS, 128])

        conv_bank = [pb(f"conv_bank{i}") for i in range(BANKS)]
        turn_bank = pb("turn_bank")
        h_bank = pb("h_bank")
        k_bank = pb("k_bank")
        q_bank = pb("q_bank")
        read_bank = pb("read_bank")
        score_bank = [q_bank, k_bank]
        gate_out = turn_bank[0:HALF, 0:TILES * E].rearrange("p (j e) -> p j e", e=E)
        rank_out = turn_bank[0:HALF, 64:64 + (TILES + 1) * E].rearrange("p (j e) -> p j e", e=E)
        table_out = q_bank[0:1, 0:2 * TABLE].rearrange("p (r n) -> p r n", r=2)

        slot_bank = conv_bank + [h_bank, q_bank, k_bank, read_bank, turn_bank]

        def tiles_of(bank, n=TILES):
            return bank[0:HALF, 0:n * 128].rearrange("p (j c) -> p j c", c=128)

        taps_in = sem("taps_in")
        weights_in = sem("weights_in")
        values_scaled = sem("values_scaled")
        late_in = sem("late_in")
        ident_ready = sem("ident_ready")
        consts_made = sem("consts_made")
        const_steps = sem("const_steps")
        tokw_turned = sem("tokw_turned")
        tokw_ready = sem("tokw_ready")
        x_loaded = [sem(f"x_loaded{i}") for i in range(2)]
        x_turned = sem("x_turned")
        xT_ready = sem("xT_ready")
        conv_mm = sem("conv_mm")
        conv_tanh = sem("conv_tanh")
        conv_mul = sem("conv_mul")
        pool_sum = sem("pool_sum")
        vector_sum = sem("vector_sum")
        h_ready = sem("h_ready")
        h_turned = sem("h_turned")
        stats1_ready = sem("stats1_ready")
        moments1_ready = sem("moments1_ready")
        norm1_steps = sem("norm1_steps")
        rstd1_ready = sem("rstd1_ready")
        m_ready = sem("m_ready")
        hm_ready = sem("hm_ready")
        m_turned = sem("m_turned")
        mT_ready = sem("mT_ready")
        q_mm = sem("q_mm")
        k_mm = sem("k_mm")
        v_mm = sem("v_mm")
        q_ready = sem("q_ready")
        k_ready = sem("k_ready")
        v_ready = sem("v_ready")
        scores_mm = [sem(f"scores_mm{b}") for b in range(PER)]
        max_ready = [sem(f"max_ready{b}") for b in range(PER)]
        probs_ready = [sem(f"probs_ready{b}") for b in range(PER)]
        rden_ready = sem("rden_ready")
        vs_ready = sem("vs_ready")
        read_mm = sem("read_mm")
        h2_ready = sem("h2_ready")
        stats2_ready = sem("stats2_ready")
        moments2_ready = sem("moments2_ready")
        norm2_steps = sem("norm2_steps")
        rstd2_ready = sem("rstd2_ready")
        xf_ready = sem("xf_ready")
        xf_turned = sem("xf_turned")
        xfT_ready = sem("xfT_ready")
        gate_mm = sem("gate_mm")
        choice_steps = sem("choice_steps")
        onehot_ready = sem("onehot_ready")
        rank_mm = sem("rank_mm")
        place_steps = sem("place_steps")
        base_ready = sem("base_ready")
        place_ready = sem("place_ready")
        token_written = sem("token_written")
        token_next = sem("token_next")
        routed_out = [sem(f"routed_out{i}") for i in range(2)]
        padding_made = sem("padding_made")
        padding_out = sem("padding_out")
        table_steps = sem("table_steps")
        table_turned = sem("table_turned")
        ends_ready = sem("ends_ready")
        table_ready = sem("table_ready")
        slot_loaded = [sem(f"slot_loaded{i}") for i in range(RING)]
        xs_ready = sem("xs_ready")
        token_at_ready = sem("token_at_ready")
        xs_turned = sem("xs_turned")
        xsT_ready = sem("xsT_ready")
        layer1_mm = sem("layer1_mm")
        hid_ready = sem("hid_ready")
        hid_turned = sem("hid_turned")
        hidT_ready = sem("hidT_ready")
        layer2_mm = sem("layer2_mm")
        done_ready = sem("done_ready")
        done_out = [sem(f"done_out{i}") for i in range(OUTS)]

        CONSTS = 16

        block = ctx.enter_context(nc.Block())

        LAST_LAG = 4
        STEPS = GROUPS + LAST_LAG
        PEELED = 6

        def run_part1(eng, step):
            for s in range(PEELED):
                step(Turn(0, 2, s), s)
            loops = (GROUPS - PEELED) // 2
            with eng.Fori(0, loops) as i:
                for c in range(2):
                    step(Turn(i, 2, PEELED + c), None)
            for s in range(PEELED + 2 * loops, STEPS):
                step(Turn(0, 2, s), s)

        def in_groups(s, lag):
            return s is None or lag <= s < GROUPS + lag

        LAST_LAG2 = 5
        STEPS2 = SLOTS + LAST_LAG2
        PEELED2 = 12

        def run_part2(eng, step, experts=None, first=0, n=0):
            for s in range(PEELED2):
                step(Turn(0, RING, s), s)
            loops = (SLOTS - PEELED2) // RING
            with eng.Fori(0, loops) as i:
                if experts:
                    experts.load(Turn(i, RING, PEELED2 + -first), n)
                for c in range(RING):
                    step(Turn(i, RING, PEELED2 + c), None)
            for s in range(PEELED2 + RING * loops, STEPS2):
                step(Turn(0, RING, s), s)

        def in_slots(s, lag):
            return s is None or lag <= s < SLOTS + lag

        def write_padding(queue, first):
            queue.wait_ge(ends_ready, 1)
            for e in range(first, E, 2):
                end = queue.value_load(row_end[0:1, e:e + 1], min_val=e * REGION, max_val=e * REGION + N)
                queue.dma_start(routed[bass.ds(end, 128), :], padding_rows[:, :]).then_inc(padding_out, 16)

        class Column:

            def __init__(self, eng, row, max_val, n=8):
                self.eng, self.row, self.max_val, self.n = eng, row, max_val, n
                self.known = {}
                self.loads = 0

            def load(self, first, n):
                regs = [self.eng.alloc_register(f"row{self.row}_{self.loads}_{i}") for i in range(n)]
                self.loads += 1
                at = first.count(1)
                self.eng.load(regs, table[0:1, self.row, slice(at, at + n) if isinstance(at, int) else bass.ds(at, n)])
                for i, reg in enumerate(regs):
                    self.known[id(first.loop), first.offset + i] = self.eng.snap(reg, donate=True, min_val=0,
                                                                                max_val=self.max_val)

            def of(self, j):
                key = (id(j.loop), j.offset)
                if key not in self.known:
                    self.load(Turn(0, RING, j.offset // self.n * self.n), self.n)
                return self.known[key]

        @block.sync
        def _(sp):
            sp.dma_start(tokw_raw[:, :], tok_w.rearrange("d c k -> d (c k)")).then_inc(taps_in, 16)
            for g in range(2):
                sp.dma_start(x_in[:, g], x_rows[g * PER * TX:(g + 1) * PER * TX, :]
                             .rearrange("(j p) c -> p j c", p=128)).then_inc(x_loaded[g], 16)
            for dst, src in ((wq_s, wq), (wk_s, wk), (wv_s, wv), (wg_s, wg)):
                sp.dma_start(dst[:, :], src).then_inc(weights_in, 16)
            for dst, src in ((bq_s, bq), (bk_s, bk)):
                sp.dma_start(dst[:, :], src.rearrange("(p a) -> p a", a=1)).then_inc(weights_in, 16)
            sp.dma_start(bv_s[:, :], bv.rearrange("(a n) -> a n", a=1).to_broadcast((128, D))).then_inc(weights_in, 16)
            sp.dma_start(bg_s[:, :], bg.rearrange("(a n) -> a n", a=1).to_broadcast((128, E))).then_inc(weights_in, 16)
            sp.dma_start(w1_s[:, :, :], w1.rearrange("e d h -> d e h")).then_inc(late_in, 16)
            for n in range(HC):
                sp.dma_start(w2_s[:, :, n, :], w2[:, n * 128:(n + 1) * 128, :].rearrange("e p d -> p e d"))\
                  .then_inc(late_in, 16)
            sp.dma_start(b1_s[:, :, :].rearrange("p e h -> p (e h)"),
                         b1.rearrange("(a e) h -> a (e h)", a=1).to_broadcast((128, E * H))).then_inc(late_in, 16)
            sp.dma_start(b2_s[:, :, :], b2.unsqueeze(0).to_broadcast((128, E, D))).then_inc(late_in, 16)
            sp.wait_ge(padding_made, 2)
            sp.dma_start(routed[PADDING:PADDING + 128, :], padding_rows[:, :]).then_inc(padding_out, 16)

            def load_x(g):
                sp.wait_ge(x_turned, g.count(1, -1))
                sp.dma_start(x_in[:, g.of(2)], x_rows[bass.ds(g.count(PER * TX), PER * TX), :]
                             .rearrange("(j p) c -> p j c", p=128)).then_inc(x_loaded[g.of(2)], 16)

            with sp.Fori(1, GROUPS // 2) as i:
                for c in range(2):
                    load_x(Turn(i, 2, c))

            write_padding(sp, 0)

            sp.wait_ge(table_ready, 1)
            sp.wait_ge(padding_out, 16 * (E + 1))
            for n in range(2):
                sp.wait_ge(routed_out[n], 16 * TILES * GROUPS // 2)

            rows_at = Column(sp, 0, PADDING)

            def load_slot(j):
                if j.at_least(RING):
                    sp.wait_ge(token_at_ready, j.count(1, 1 - RING))
                at = rows_at.of(j)
                sp.dma_start(tl[:, j.of(RING)], routed[bass.ds(at, 128), :]).then_inc(slot_loaded[j.of(RING)], 16)

            for j in range(RING):
                load_slot(Turn(0, RING, j))
            with sp.Fori(1, SLOTS // RING) as i:
                rows_at.load(Turn(i, RING, 0), RING)
                for c in range(RING):
                    load_slot(Turn(i, RING, c))
            for j in range(SLOTS // RING * RING, SLOTS):
                load_slot(Turn(0, RING, j))

        @block.gpsimd
        def _(pool):
            pool.memset(ident[:, :], 0.0).then_inc(const_steps, 1)
            pool.wait_ge(const_steps, 1)
            pool.affine_select(out=ident[:, :], in_=ident[:, :], compare_op=ALU.not_equal, fill=1.0, base=0,
                               pattern=[[-1, 128]], channel_multiplier=1).then_inc(ident_ready, 1)
            pool.memset(mask_bf[:, :], 0.0).then_inc(const_steps, 1)
            pool.memset(before_bf[:, :], 1.0).then_inc(const_steps, 1)
            pool.memset(padding_rows[:, 0:TOKEN], 0.0).then_inc(padding_made, 1)
            pool.memset(padding_rows[:, TOKEN:ROW].bitcast(UINT32), NOWHERE).then_inc(padding_made, 1)
            pool.memset(ones_bf[:, :], 1.0).then_inc(consts_made, 1)
            pool.memset(onehot[:, :, TILES, :], 0.0).then_inc(consts_made, 1)
            pool.memset(eps_s[:, :], EPS).then_inc(consts_made, 1)
            pool.memset(power_s[:, :], -0.5).then_inc(consts_made, 1)
            pool.memset(zero_s[:, :], 0.0).then_inc(consts_made, 1)
            pool.memset(zero_u[:, :], 0).then_inc(consts_made, 1)
            pool.memset(group_step[:, :], GT).then_inc(consts_made, 1)
            pool.memset(ones_e[:, :], 1.0).then_inc(consts_made, 1)
            pool.iota(ramp[:, :], [[-1, E]], base=E, channel_multiplier=0,
                      allow_small_or_imprecise_dtypes=True).then_inc(consts_made, 1)
            pool.iota(next_token[:, :], [[HALF, TILES]], base=0, channel_multiplier=1).then_inc(consts_made, 1)
            pool.iota(base[:, :], [[REGION, E]], base=0, channel_multiplier=0,
                      allow_small_or_imprecise_dtypes=True).then_inc(consts_made, 1)
            pool.iota(region_up[:, :], [[REGION, E]], base=-127, channel_multiplier=0,
                      allow_small_or_imprecise_dtypes=True).then_inc(consts_made, 1)
            pool.iota(slot_no[:, :], [[0, E]], base=0, channel_multiplier=1,
                      allow_small_or_imprecise_dtypes=True).then_inc(consts_made, 1)
            pool.iota(skipped[:, E:E + 1], [[0, 1]], base=0, channel_multiplier=128,
                      allow_small_or_imprecise_dtypes=True).then_inc(consts_made, 1)
            pool.wait_ge(const_steps, 3)
            pool.affine_select(out=mask_bf[:, :], in_=mask_bf[:, :], compare_op=ALU.is_ge, fill=MASKED, base=0,
                               pattern=[[1, HALF]], channel_multiplier=-1).then_inc(consts_made, 1)
            pool.affine_select(out=before_bf[:, :], in_=before_bf[:, :], compare_op=ALU.is_gt, fill=0.0, base=0,
                               pattern=[[1, HALF]], channel_multiplier=-1).then_inc(consts_made, 1)
            pool.wait_ge(consts_made, CONSTS)

            def normal(mean, var, moments_ready, steps, rstd_ready, g):
                pool.wait_ge(moments_ready, g.count(1, 1))
                pool.tensor_tensor(var, var, eps_s[0:HALF, :], ALU.add).then_inc(steps, 1)
                pool.tensor_tensor(mean, zero_s[0:HALF, :], mean, ALU.subtract).then_inc(steps, 1)
                pool.wait_ge(steps, g.count(3, 1))
                pool.tensor_tensor(var, var, power_s[0:HALF, :], ALU.pow).then_inc(steps, 1)
                pool.wait_ge(steps, g.count(3, 3))
                pool.tensor_tensor(mean, mean, var, ALU.mult).then_inc(rstd_ready, 1)

            def norm_h(g):
                normal(norm1[0:HALF, g.of(2), :, 0], norm1[0:HALF, g.of(2), :, 1], moments1_ready, norm1_steps,
                       rstd1_ready, g)

            def norm_h2(g):
                normal(rows[0:HALF, g.of(2), :, SHIFT], rows[0:HALF, g.of(2), :, RSTD], moments2_ready, norm2_steps,
                       rstd2_ready, g)

            def sum_tap(g, k):
                pool.wait_ge(conv_mul, g.count(TAPS, k + 1))
                if k > 1:
                    pool.wait_ge(pool_sum, g.count(3, k - 1))
                pool.tensor_tensor(prod[:, g.of(2), 0], prod[:, g.of(2), 0], prod[:, g.of(2), k], ALU.add)\
                    .then_inc(pool_sum, 1)

            def route(g):
                if g.at_least(2):
                    pool.wait_ge(routed_out[g.of(2)], g.uses(2, 16 * TILES))
                if g.at_least(1):
                    pool.wait_ge(token_next, g.count(1))
                pool.tensor_tensor(rows[0:HALF, g.of(2), :, TOKEN].bitcast(UINT32), next_token[0:HALF, :],
                                   zero_u[0:HALF, :], ALU.add).then_inc(token_written, 1)
                pool.wait_ge(token_written, g.count(1, 1))
                pool.wait_ge(place_ready, g.count(1, 1))
                pool.tensor_tensor(next_token[:, :], next_token[:, :], group_step[:, :], ALU.add)\
                    .then_inc(token_next, 1)
                for j in range(TILES):
                    pool.indirect_dma_start(
                        out=routed, out_offset=bass.IndirectOffsetOnAxis(ap=row_at[0:HALF, g.of(2), j:j + 1], axis=0),
                        in_=rows[0:HALF, g.of(2), j, :], in_offset=None).then_inc(routed_out[g.of(2)], 16)

            def step(t, s):
                if in_groups(s, 1):
                    norm_h(t + -1)
                if in_groups(s, 0):
                    sum_tap(t, 1)
                    sum_tap(t, 2)
                    sum_tap(t, 3)
                if in_groups(s, 2):
                    norm_h2(t + -2)
                if in_groups(s, 3):
                    route(t + -3)

            run_part1(pool, step)

            def step2(t, s):
                if in_slots(s, 5):
                    pool.wait_ge(done_ready, t.count(1, -4))
                    pool.wait_ge(token_at_ready, t.count(1, -4))
                if in_slots(s, 4):
                    j = t + -4
                    if s == 4:
                        pool.wait_ge(hid_ready, 1)
                    pool.tensor_tensor(token_at[:, j.of(RING):j.of(RING) + 1],
                                       tl[:, j.of(RING), TOKEN:ROW].bitcast(UINT32),
                                       zero_u[:, 0:1], ALU.add).then_inc(token_at_ready, 1)
                if in_slots(s, 5):
                    j = t + -5
                    pool.indirect_dma_start(
                        out=out_rows,
                        out_offset=bass.IndirectOffsetOnAxis(ap=token_at[:, j.of(RING):j.of(RING) + 1], axis=0),
                        in_=done_rows[:, j.of(OUTS)], in_offset=None,
                        bounds_check=N - 1, oob_is_err=False).then_inc(done_out[j.of(OUTS)], 16)

            run_part2(pool, step2)
            for n in range(OUTS):
                pool.wait_ge(done_out[n], 16 * len(range(n, SLOTS, OUTS)))

        @block.scalar
        def _(act):
            for n in range(2):
                act.wait_ge(tokw_turned, n + 1)
                src = conv_bank[n][:, :].rearrange("p (k d) -> p k d", d=D)
                take = min(4, TAPS - 4 * n)
                act.activation(tokw[:, 4 * n:4 * n + take, :], src[:, 0:take, :], ACT.Copy).then_inc(tokw_ready, 1)

            def copy_xT(g):
                act.wait_ge(x_turned, g.count(1, 1))
                if g.at_least(2):
                    act.wait_ge(conv_mul, g.count(TAPS, -TAPS))
                act.activation(xT[:, g.of(2)].rearrange("p b t -> p (b t)"), turn_bank[:, :], ACT.Copy)\
                    .then_inc(xT_ready, 1)

            def tanh(g, k):
                act.wait_ge(conv_mm, g.count(TAPS, k + 1))
                bank = conv_bank[(k + g.of(2)) % BANKS][:, 0:GT]
                act.activation(bank, bank, ACT.Tanh).then_inc(conv_tanh, 1)

            def normalize_h(g):
                act.wait_ge(rstd1_ready, g.count(1, 1))
                if g.at_least(2):
                    act.wait_ge(hm_ready, g.count(1, -1))
                    act.wait_ge(m_turned, g.count(1, -1))
                for j in range(TILES):
                    ins = act.activation(m[0:HALF, g.of(2), j, :], tiles_of(h_bank)[:, j, :], ACT.Identity,
                                         bias=norm1[0:HALF, g.of(2), j, 0:1], scale=norm1[0:HALF, g.of(2), j, 1:2])
                ins.then_inc(m_ready, 1)

            def copy_mT(g):
                act.wait_ge(m_turned, g.count(1, 1))
                if g.at_least(2):
                    act.wait_ge(q_mm, g.count(1, -1))
                    act.wait_ge(k_mm, g.count(1, -1))
                    act.wait_ge(v_mm, g.count(1, -1))
                act.activation(mT[:, g.of(2)].rearrange("p j t -> p (j t)"), h_bank[:, 0:GT], ACT.Copy)\
                    .then_inc(mT_ready, 1)

            def add_bias(dst, bank, bias, mm, ready, g):
                act.wait_ge(mm, g.count(1, 1))
                if g.at_least(2):
                    for b in range(PER):
                        act.wait_ge(scores_mm[b], g.count(1, -1))
                act.activation(dst[:, g.of(2)].rearrange("p b t -> p (b t)"), bank[:, 0:GT], ACT.Identity,
                               bias=bias[:, 0:1]).then_inc(ready, 1)

            def add_bq(g):
                add_bias(qT, q_bank, bq_s, q_mm, q_ready, g)

            def add_bk(g):
                add_bias(kT, k_bank, bk_s, k_mm, k_ready, g)

            def exps(g, b):
                act.wait_ge(max_ready[b], g.count(1, 1))
                if g.at_least(2):
                    act.wait_ge(read_mm, g.count(1, -1))
                    act.wait_ge(rden_ready, g.count(1, -1))
                for n, (lo, hi) in enumerate(((0, L), (L, L + HALF))):
                    n += 2 * b
                    ins = act.activation(probs[0:HALF, g.of(2), b, lo:hi], score_bank[b][0:HALF, lo:hi], ACT.Exp,
                                         bias=neg_max[0:HALF, g.of(2), n:n + 1],
                                         accum_out=den[0:HALF, g.of(2), n:n + 1])
                ins.then_inc(probs_ready[b], 1)

            def scale_values(g):
                act.wait_ge(rden_ready, g.count(1, 1))
                act.wait_ge(v_ready, g.count(1, 1))
                if g.at_least(2):
                    act.wait_ge(read_mm, g.count(1, -1))
                for j in range(TILES):
                    ins = act.activation(vs[0:HALF, g.of(2), j, :], vb[0:HALF, g.of(2), j, :], ACT.Copy,
                                         scale=rden[0:HALF, g.of(2), j:j + 1])
                ins.then_inc(vs_ready, 1)

            def normalize_h2(g):
                act.wait_ge(rstd2_ready, g.count(1, 1))
                if g.at_least(2):
                    act.wait_ge(xf_turned, g.count(1, -1))
                rr = rows[0:HALF, g.of(2)]
                for j in range(TILES):
                    ins = act.activation(xf[0:HALF, g.of(2), j, :], rr[:, j, 0:D], ACT.Identity,
                                         bias=rr[:, j, SHIFT:SHIFT + 1], scale=rr[:, j, RSTD:RSTD + 1])
                ins.then_inc(xf_ready, 1)

            def copy_xfT(g):
                act.wait_ge(xf_turned, g.count(1, 1))
                if g.at_least(2):
                    act.wait_ge(gate_mm, g.count(1, -1))
                act.activation(xfT[:, g.of(2)].rearrange("p j t -> p (j t)"), turn_bank[:, 0:GT], ACT.Copy)\
                    .then_inc(xfT_ready, 1)

            def scale_values_weights():
                act.wait_ge(weights_in, 16 * 8)
                act.activation(wv_s[:, :], wv_s[:, :], ACT.Copy, scale=READ_SCALE).then_inc(values_scaled, 1)
                act.activation(bv_s[:, :], bv_s[:, :], ACT.Copy, scale=READ_SCALE).then_inc(values_scaled, 1)

            def step(t, s):
                if s == 1:
                    scale_values_weights()
                if in_groups(s, 0):
                    copy_xT(t)
                if in_groups(s, 2):
                    copy_mT(t + -2)
                if in_groups(s, 1):
                    tanh(t + -1, 6)
                if in_groups(s, 2):
                    add_bq(t + -2)
                if in_groups(s, 0):
                    tanh(t, 0)
                if in_groups(s, 2):
                    add_bk(t + -2)
                if in_groups(s, 0):
                    tanh(t, 1)
                if in_groups(s, 3):
                    normalize_h2(t + -3)
                if in_groups(s, 0):
                    tanh(t, 2)
                if in_groups(s, 2):
                    exps(t + -2, 1)
                    exps(t + -2, 0)
                if in_groups(s, 3):
                    copy_xfT(t + -3)
                if in_groups(s, 2):
                    scale_values(t + -2)
                if in_groups(s, 0):
                    tanh(t, 3)
                    tanh(t, 4)
                if in_groups(s, 1):
                    normalize_h(t + -1)
                if in_groups(s, 0):
                    tanh(t, 5)

            run_part1(act, step)
            write_padding(act, 1)

            def step2(t, s):
                if in_slots(s, 1):
                    j = t + -1
                    act.wait_ge(xs_turned, j.count(1, 1))
                    act.activation(xsT[:, j.of(2)], slot_bank[j.of(8)][:, 0:D], ACT.Copy).then_inc(xsT_ready, 1)
                if in_slots(s, 0):
                    j = t
                    act.wait_ge(slot_loaded[j.of(RING)], j.uses(RING, 16, 16))
                    row = tl[:, j.of(RING)]
                    act.activation(xs[:, j.of(2)], row[:, 0:D], ACT.Identity, bias=row[:, SHIFT:SHIFT + 1],
                                   scale=row[:, RSTD:RSTD + 1]).then_inc(xs_ready, 1)
                if in_slots(s, 3):
                    j = t + -3
                    act.wait_ge(hid_turned, j.count(1, 1))
                    act.activation(hidT[:, j.of(2)], slot_bank[j.of(8)][:, 0:H], ACT.Relu).then_inc(hidT_ready, 1)

            run_part2(act, step2)

        @block.vector
        def _(dve):
            dve.wait_ge(consts_made, CONSTS)
            dve.wait_ge(ident_ready, 1)
            dve.tensor_copy(ident_bf[:, :], ident[:, :]).then_inc(consts_made, 1)

            def mul(g, k):
                dve.wait_ge(conv_tanh, g.count(TAPS, k + 1))
                if k == 0 and g.at_least(2):
                    dve.wait_ge(h_ready, g.count(1, -1))
                w = conv_bank[(k + g.of(2)) % BANKS][:, 0:GT].rearrange("p (b t) -> p b t", b=PER)
                dve.tensor_tensor(prod[:, g.of(2), k].rearrange("p (b t) -> p b t", b=PER), w,
                                  xT[:, g.of(2), :, k:k + L], ALU.mult).then_inc(conv_mul, 1)

            def add_tap5(g):
                dve.wait_ge(conv_mul, g.count(TAPS, 6))
                dve.tensor_tensor(prod[:, g.of(2), 4], prod[:, g.of(2), 4], prod[:, g.of(2), 5], ALU.add)\
                    .then_inc(vector_sum, 1)

            def add_tap6(g):
                dve.wait_ge(conv_mul, g.count(TAPS, 7))
                dve.wait_ge(vector_sum, g.count(2, 1))
                dve.tensor_tensor(prod[:, g.of(2), 4], prod[:, g.of(2), 4], prod[:, g.of(2), 6], ALU.add)\
                    .then_inc(vector_sum, 1)

            def add_h(g):
                dve.wait_ge(vector_sum, g.count(2, 2))
                dve.wait_ge(pool_sum, g.count(3, 3))
                if g.at_least(2):
                    dve.wait_ge(h_turned, g.count(1, -1))
                dve.tensor_tensor(hT[:, g.of(2)].rearrange("p j t -> p (j t)"), prod[:, g.of(2), 0],
                                  prod[:, g.of(2), 4], ALU.add).then_inc(h_ready, 1)

            def stats_h(g):
                dve.wait_ge(h_turned, g.count(1, 1))
                for j in range(TILES):
                    ins = dve.bn_stats(stats1[0:HALF, j, :], tiles_of(h_bank)[:, j, :])
                ins.then_inc(stats1_ready, 1)

            def moments_h(g):
                for j in range(TILES):
                    ins = dve.bn_aggr(norm1[0:HALF, g.of(2), j, :], stats1[0:HALF, j, :])
                ins.then_inc(moments1_ready, 1)

            def add_m(g):
                dve.wait_ge(m_ready, g.count(1, 1))
                if g.at_least(2):
                    dve.wait_ge(h2_ready, g.count(1, -1))
                dve.tensor_tensor(hm[0:HALF, g.of(2)], tiles_of(h_bank), m[0:HALF, g.of(2)], ALU.add)\
                    .then_inc(hm_ready, 1)

            def add_bv(g):
                dve.wait_ge(v_mm, g.count(1, 1))
                if g.at_least(2):
                    dve.wait_ge(vs_ready, g.count(1, -1))
                dve.tensor_tensor(vb[0:HALF, g.of(2)], tiles_of(read_bank),
                                  bv_s[0:HALF].unsqueeze(1).to_broadcast((HALF, TILES, D)), ALU.add)\
                    .then_inc(v_ready, 1)

            def maxima(g, b):
                dve.wait_ge(scores_mm[b], g.count(1, 1))
                if g.at_least(2):
                    dve.wait_ge(probs_ready[b], g.count(1, -1))
                for n, (lo, hi) in enumerate(((0, L), (L, L + HALF))):
                    n += 2 * b
                    ins = dve.tensor_reduce(neg_max[0:HALF, g.of(2), n:n + 1], score_bank[b][0:HALF, lo:hi],
                                            axis=AX.X, op=ALU.max, negate=True)
                ins.then_inc(max_ready[b], 1)

            def divide(g):
                for b in range(PER):
                    dve.wait_ge(probs_ready[b], g.count(1, 1))
                if g.at_least(2):
                    dve.wait_ge(vs_ready, g.count(1, -1))
                dve.reciprocal(rden[0:HALF, g.of(2)], den[0:HALF, g.of(2)]).then_inc(rden_ready, 1)

            def add_read(g):
                dve.wait_ge(read_mm, g.count(1, 1))
                dve.wait_ge(hm_ready, g.count(1, 1))
                if g.at_least(2):
                    dve.wait_ge(routed_out[g.of(2)], g.uses(2, 16 * TILES))
                dve.tensor_tensor(rows[0:HALF, g.of(2), :, 0:D], tiles_of(read_bank), hm[0:HALF, g.of(2)], ALU.add)\
                    .then_inc(h2_ready, 1)

            def stats_h2(g):
                dve.wait_ge(h2_ready, g.count(1, 1))
                for j in range(TILES):
                    ins = dve.bn_stats(stats2[0:HALF, j, :], rows[0:HALF, g.of(2), j, 0:D])
                ins.then_inc(stats2_ready, 1)

            def moments_h2(g):
                for j in range(TILES):
                    ins = dve.bn_aggr(rows[0:HALF, g.of(2), j, SHIFT:SHIFT + 2], stats2[0:HALF, j, :])
                ins.then_inc(moments2_ready, 1)

            def choose(g):
                dve.wait_ge(gate_mm, g.count(1, 1))
                dve.tensor_tensor(logits[0:HALF], gate_out, bg_s[0:HALF].unsqueeze(1).to_broadcast((HALF, TILES, E)),
                                  ALU.add).then_inc(choice_steps, 1)
                dve.wait_ge(choice_steps, g.count(5, 1))
                dve.tensor_reduce(top[0:HALF], logits[0:HALF], axis=AX.X, op=ALU.max).then_inc(choice_steps, 1)
                dve.wait_ge(choice_steps, g.count(5, 2))
                dve.tensor_tensor(is_top[0:HALF], logits[0:HALF],
                                  top[0:HALF].unsqueeze(2).to_broadcast((HALF, TILES, E)), ALU.is_equal)\
                    .then_inc(choice_steps, 1)
                dve.wait_ge(choice_steps, g.count(5, 3))
                dve.tensor_tensor(top_ramp[0:HALF], is_top[0:HALF],
                                  ramp[0:HALF].unsqueeze(1).to_broadcast((HALF, TILES, E)), ALU.mult)\
                    .then_inc(choice_steps, 1)
                dve.wait_ge(choice_steps, g.count(5, 4))
                dve.tensor_reduce(first[0:HALF], top_ramp[0:HALF], axis=AX.X, op=ALU.max).then_inc(choice_steps, 1)
                dve.wait_ge(choice_steps, g.count(5, 5))
                if g.at_least(2):
                    dve.wait_ge(rank_mm, g.count(1, -1))
                dve.tensor_tensor(onehot[0:HALF, g.of(2), 0:TILES], ramp[0:HALF].unsqueeze(1).to_broadcast((HALF, TILES, E)),
                                  first[0:HALF].unsqueeze(2).to_broadcast((HALF, TILES, E)), ALU.is_equal)\
                    .then_inc(onehot_ready, 1)

            def places(g):
                dve.wait_ge(rank_mm, g.count(1, 1))
                if g.at_least(1):
                    dve.wait_ge(base_ready, g.count(1))
                dve.tensor_tensor(place[0:HALF], rank_out[:, 0:TILES], base[0:HALF].unsqueeze(1).to_broadcast((HALF, TILES, E)),
                                  ALU.add).then_inc(place_steps, 1)
                dve.wait_ge(place_steps, g.count(3, 1))
                dve.tensor_tensor(base[0:HALF], base[0:HALF], rank_out[:, TILES], ALU.add).then_inc(base_ready, 1)
                dve.tensor_tensor(place1[0:HALF], place[0:HALF], onehot[0:HALF, g.of(2), 0:TILES], ALU.mult)\
                    .then_inc(place_steps, 1)
                dve.wait_ge(place_steps, g.count(3, 2))
                dve.tensor_reduce(row_sum[0:HALF], place1[0:HALF], axis=AX.X, op=ALU.add).then_inc(place_steps, 1)
                dve.wait_ge(place_steps, g.count(3, 3))
                if g.at_least(2):
                    dve.wait_ge(routed_out[g.of(2)], g.uses(2, 16 * TILES))
                dve.tensor_copy(row_at[0:HALF, g.of(2)], row_sum[0:HALF]).then_inc(place_ready, 1)

            def step(t, s):
                if in_groups(s, 3):
                    add_bv(t + -3)
                if in_groups(s, 2):
                    dve.wait_ge(stats1_ready, (t + -2).count(1, 1))
                if in_groups(s, 3):
                    divide(t + -3)
                if in_groups(s, 2):
                    moments_h(t + -2)
                if in_groups(s, 1):
                    mul(t + -1, 2)
                if in_groups(s, 4):
                    choose(t + -4)
                if in_groups(s, 1):
                    mul(t + -1, 3)
                    mul(t + -1, 4)
                if in_groups(s, 3):
                    add_read(t + -3)
                if in_groups(s, 2):
                    add_m(t + -2)
                if in_groups(s, 3):
                    stats_h2(t + -3)
                if in_groups(s, 3):
                    dve.wait_ge(stats2_ready, (t + -3).count(1, 1))
                if in_groups(s, 1):
                    mul(t + -1, 5)
                if in_groups(s, 3):
                    moments_h2(t + -3)
                if in_groups(s, 1):
                    add_tap5(t + -1)
                    mul(t + -1, 6)
                if in_groups(s, 4):
                    places(t + -4)
                if in_groups(s, 1):
                    add_tap6(t + -1)
                if in_groups(s, 0):
                    mul(t, 0)
                if in_groups(s, 1):
                    add_h(t + -1)
                if in_groups(s, 0):
                    mul(t, 1)
                if in_groups(s, 2):
                    maxima(t + -2, 1)
                    maxima(t + -2, 0)
                if in_groups(s, 1):
                    stats_h(t + -1)

            run_part1(dve, step)

            done = [0]

            def then(ins):
                done[0] += 1
                ins.then_inc(table_steps, 1)
                dve.wait_ge(table_steps, done[0])

            dve.wait_ge(base_ready, GROUPS)
            dve.tensor_copy(row_end[:, :], base[0:1, :]).then_inc(ends_ready, 1)
            then(dve.tensor_tensor(held_up[:, :], base[0:TABLE, :], region_up[:, :], ALU.subtract))
            then(dve.tensor_single_scalar(tiles_i[:, :], held_up[:, :], 7, ALU.arith_shift_right))
            then(dve.tensor_copy(tiles_f[:, :], tiles_i[:, :]))
            then(dve.tensor_tensor_scan(tile_end[:, :], ones_e[:, :], tiles_f[:, :], 0.0, ALU.mult, ALU.add))
            then(dve.tensor_tensor(ended[:, :], slot_no[:, :], tile_end[:, :], ALU.is_ge))
            then(dve.tensor_scalar(skip[:, :], tiles_f[:, :], -128.0, float(REGION), ALU.mult, ALU.add))
            then(dve.tensor_tensor(skipped[:, 0:E], ended[:, :], skip[:, :], ALU.mult))
            dve.tensor_reduce(slot_at[:, 0:1], skipped[:, :], axis=AX.X, op=ALU.add)
            then(dve.tensor_reduce(slot_at[:, 1:2], ended[:, :], axis=AX.X, op=ALU.add))
            dve.wait_ge(table_turned, 1)
            dve.tensor_scalar(table[:, 0, :], table_out[:, 0, :], float(PADDING), None, ALU.min)
            dve.tensor_scalar(table[:, 1, :], table_out[:, 1, :], float(E - 1), None, ALU.min).then_inc(table_ready, 1)
            dve.wait_ge(table_ready, 1)
            experts = Column(dve, 1, E - 1)

            dve.wait_ge(late_in, 16 * (3 + HC))

            def step2(t, s):
                if in_slots(s, 5):
                    j = t + -5
                    dve.wait_ge(layer2_mm, j.count(1, 1))
                    if j.at_least(OUTS):
                        dve.wait_ge(done_out[j.of(OUTS)], j.uses(OUTS, 16))
                    dve.tensor_tensor(done_rows[:, j.of(OUTS)], slot_bank[j.of(8)][:, D + H:2 * D + H], res[:, j.of(RING)], ALU.add)\
                        .then_inc(done_ready, 1)
                if in_slots(s, 2):
                    j = t + -2
                    e = experts.of(j)
                    dve.wait_ge(layer1_mm, j.count(1, 1))
                    dve.tensor_tensor(res[:, j.of(RING)], tl[:, j.of(RING), 0:D],
                                      b2_s[:, bass.ds(e, 1), :].rearrange("p a d -> p (a d)"), ALU.add)
                    dve.tensor_tensor(hid[:, j.of(2)], slot_bank[j.of(8)][:, D:D + H],
                                      b1_s[:, bass.ds(e, 1), :].rearrange("p a h -> p (a h)"), ALU.add)\
                        .then_inc(hid_ready, 1)

            run_part2(dve, step2, experts, 2, RING)

        @block.tensor
        def _(pe):
            pe.wait_ge(taps_in, 16)
            pe.wait_ge(ident_ready, 1)
            raw = tokw_raw[:, :].rearrange("d (c k) -> d k c", k=TAPS)
            for k in range(TAPS):
                ins = pe.transpose(conv_bank[k // 4][:, k % 4 * 128:(k % 4 + 1) * 128], raw[:, k, :], ident[:, :])
                if k == 3 or k == TAPS - 1:
                    ins.then_inc(tokw_turned, 1)

            def bank_free(users, g):
                if not isinstance(g.loop, int):
                    taken, ahead = users[0]
                    pe.wait_ge(taken, g.count(1, ahead + 1))
                    return
                for taken, ahead in users:
                    if min(g.offset + ahead, GROUPS - 1) >= 0:
                        pe.wait_ge(taken, min(g.offset + ahead, GROUPS - 1) + 1)

            def turn_x(g):
                bank_free([(onehot_ready, -4), (xfT_ready, -4), (base_ready, -5), (xT_ready, -1)], g)
                pe.wait_ge(x_loaded[g.of(2)], g.uses(2, 16, 16))
                for j in range(4):
                    ins = pe.transpose(turn_bank[:, j * 128:(j + 1) * 128], x_in[:, g.of(2), j, :], ident[:, :])
                ins.then_inc(x_turned, 1)

            pe.wait_ge(tokw_ready, 2)

            def conv(g, k):
                if k == 0:
                    pe.wait_ge(xT_ready, g.count(1, 1))
                n = (k + g.of(2)) % BANKS
                if k >= BANKS:
                    pe.wait_ge(conv_mul, g.count(TAPS, k - BANKS + 1))
                elif g.at_least(1):
                    last = max(q for q in range(TAPS) if (q + 1 - g.of(2)) % BANKS == n)
                    pe.wait_ge(conv_mul, g.count(TAPS, last + 1 - TAPS))
                pe.matmul(conv_bank[n][:, 0:GT], tokw[:, k, :], xT[:, g.of(2), :, TAPS - 1:TX],
                          start=True, stop=True).then_inc(conv_mm, 1)

            def turn_h(g):
                bank_free([(mT_ready, -1), (hm_ready, -1)], g)
                pe.wait_ge(h_ready, g.count(1, 1))
                for j in range(TILES):
                    ins = pe.transpose(tiles_of(h_bank)[:, j, :], hT[:, g.of(2), j, :], ident[:, :])
                ins.then_inc(h_turned, 1)

            def turn_m(g):
                bank_free([(hm_ready, 0), (mT_ready, -1)], g)
                pe.wait_ge(m_ready, g.count(1, 1))
                for j in range(TILES):
                    ins = pe.transpose(h_bank[:, j * HALF:(j + 1) * HALF], m[0:HALF, g.of(2), j, :],
                                       ident[0:HALF, 0:HALF])
                ins.then_inc(m_turned, 1)

            def queries(g):
                bank_free([(probs_ready[0], -1), (q_ready, -1)], g)
                pe.wait_ge(mT_ready, g.count(1, 1))
                pe.matmul(q_bank[:, 0:GT], wq_s[:, :], mT[:, g.of(2)].rearrange("p j t -> p (j t)"),
                          start=True, stop=True).then_inc(q_mm, 1)

            def keys(g):
                bank_free([(probs_ready[1], -1), (k_ready, -1)], g)
                pe.wait_ge(mT_ready, g.count(1, 1))
                pe.matmul(k_bank[:, 0:GT], wk_s[:, :], mT[:, g.of(2)].rearrange("p j t -> p (j t)"),
                          start=True, stop=True).then_inc(k_mm, 1)

            def values(g):
                bank_free([(h2_ready, -1), (v_ready, -1)], g)
                pe.wait_ge(mT_ready, g.count(1, 1))
                for j in range(TILES):
                    ins = pe.matmul(tiles_of(read_bank)[:, j, :], mT[:, g.of(2), j, :], wv_s[:, :],
                                    start=True, stop=True)
                ins.then_inc(v_mm, 1)

            def scores(g, b):
                bank_free([[(q_ready, 0), (probs_ready[0], -1)], [(k_ready, 0), (probs_ready[1], -1)]][b], g)
                pe.wait_ge(q_ready, g.count(1, 1))
                pe.wait_ge(k_ready, g.count(1, 1))
                for n, (lo, hi) in enumerate(((0, L), (L, L + HALF))):
                    pe.matmul(score_bank[b][0:HALF, lo:hi], kT[:, g.of(2), b, n * HALF:(n + 1) * HALF],
                              qT[:, g.of(2), b, n * HALF:L], start=True, stop=False)
                    ins = pe.matmul(score_bank[b][0:HALF, lo:lo + HALF], ident_bf[0:HALF, 0:HALF],
                                    mask_bf[0:HALF, :], start=False, stop=True)
                ins.then_inc(scores_mm[b], 1)

            def read(g):
                bank_free([(v_ready, 0), (h2_ready, -1)], g)
                for b in range(PER):
                    pe.wait_ge(probs_ready[b], g.count(1, 1))
                pe.wait_ge(vs_ready, g.count(1, 1))
                out = tiles_of(read_bank)
                for b in range(PER):
                    p = probs[0:HALF, g.of(2), b]
                    v0, v1 = vs[0:HALF, g.of(2), 2 * b, :], vs[0:HALF, g.of(2), 2 * b + 1, :]
                    pe.matmul(out[:, 2 * b, :], p[:, 0:HALF], v0, start=True, stop=True)
                    pe.matmul(out[:, 2 * b + 1, :], p[:, HALF:L], v0, start=True, stop=False)
                    ins = pe.matmul(out[:, 2 * b + 1, :], p[:, L:L + HALF], v1, start=False, stop=True)
                ins.then_inc(read_mm, 1)

            def turn_xf(g):
                bank_free([(base_ready, -1), (xT_ready, 3), (onehot_ready, -1), (xfT_ready, -1)], g)
                pe.wait_ge(xf_ready, g.count(1, 1))
                for j in range(TILES):
                    ins = pe.transpose(turn_bank[:, j * HALF:(j + 1) * HALF], xf[0:HALF, g.of(2), j, :],
                                       ident[0:HALF, 0:HALF])
                ins.then_inc(xf_turned, 1)

            def gate(g):
                bank_free([(xfT_ready, 0), (base_ready, -1), (xT_ready, 3), (onehot_ready, -1)], g)
                pe.wait_ge(xfT_ready, g.count(1, 1))
                for j in range(TILES):
                    ins = pe.matmul(gate_out[:, j, :], xfT[:, g.of(2), j, :], wg_s[:, :], start=True, stop=True)
                ins.then_inc(gate_mm, 1)

            def ranks(g):
                bank_free([(xT_ready, 4), (onehot_ready, 0), (xfT_ready, 0), (base_ready, -1)], g)
                pe.wait_ge(onehot_ready, g.count(1, 1))
                chosen = onehot[0:HALF, g.of(2)]
                pe.matmul(rank_out, before_bf[0:HALF, :], chosen, start=True, stop=False)
                for j in range(TILES):
                    n = TILES - j
                    ins = pe.matmul(rank_out[:, j + 1:], ones_bf[0:HALF, 0:HALF],
                                    chosen[:, j:j + 1, :].to_broadcast((HALF, n, E)), start=False, stop=(n == 1))
                ins.then_inc(rank_mm, 1)

            def step(t, s):
                if s == 2:
                    pe.wait_ge(values_scaled, 2)
                    pe.wait_ge(consts_made, CONSTS + 1)
                if in_groups(s, 4):
                    gate(t + -4)
                if in_groups(s, 1):
                    conv(t + -1, 4)
                if in_groups(s, 3):
                    read(t + -3)
                if in_groups(s, 1):
                    conv(t + -1, 5)
                if in_groups(s, 0):
                    turn_x(t)
                if in_groups(s, 1):
                    conv(t + -1, 6)
                if in_groups(s, 2):
                    turn_m(t + -2)
                if in_groups(s, 0):
                    conv(t, 0)
                if in_groups(s, 4):
                    ranks(t + -4)
                if in_groups(s, 2):
                    queries(t + -2)
                    keys(t + -2)
                if in_groups(s, 0):
                    conv(t, 1)
                    conv(t, 2)
                if in_groups(s, 2):
                    scores(t + -2, 1)
                    scores(t + -2, 0)
                if in_groups(s, 1):
                    turn_h(t + -1)
                if in_groups(s, 2):
                    values(t + -2)
                if in_groups(s, 3):
                    turn_xf(t + -3)
                if in_groups(s, 0):
                    conv(t, 3)

            run_part1(pe, step)

            pe.wait_ge(table_steps, 8)
            for n in range(2):
                ins = pe.matmul(table_out[:, n, :], slot_at[:, n:n + 1], ident[0:TABLE, 0:TABLE], start=True, stop=True)
            ins.then_inc(table_turned, 1)
            pe.wait_ge(table_ready, 1)
            pe.wait_ge(late_in, 16 * (3 + HC))

            experts = Column(pe, 1, E - 1, 8)

            def step2(t, s):
                if in_slots(s, 2):
                    j = t + -2
                    e = experts.of(j)
                    pe.wait_ge(xsT_ready, j.count(1, 1))
                    pe.matmul(slot_bank[j.of(8)][:, D:D + H], xsT[:, j.of(2)],
                              w1_s[:, bass.ds(e, 1), :].rearrange("p a h -> p (a h)"), start=True, stop=True)\
                        .then_inc(layer1_mm, 1)
                if in_slots(s, 1):
                    j = t + -1
                    pe.wait_ge(xs_ready, j.count(1, 1))
                    pe.transpose(slot_bank[j.of(8)][:, 0:D], xs[:, j.of(2)], ident[:, :]).then_inc(xs_turned, 1)
                if in_slots(s, 3):
                    j = t + -3
                    pe.wait_ge(hid_ready, j.count(1, 1))
                    for n in range(HC):
                        ins = pe.transpose(slot_bank[j.of(8)][:, n * 128:(n + 1) * 128],
                                           hid[:, j.of(2), n * 128:(n + 1) * 128], ident[:, :])
                    ins.then_inc(hid_turned, 1)
                if in_slots(s, 4):
                    j = t + -4
                    e = experts.of(j)
                    pe.wait_ge(hidT_ready, j.count(1, 1))
                    for n in range(HC):
                        ins = pe.matmul(slot_bank[j.of(8)][:, D + H:2 * D + H], hidT[:, j.of(2), n * 128:(n + 1) * 128],
                                        w2_s[:, bass.ds(e, 1), n, :].rearrange("p a d -> p (a d)"),
                                        start=(n == 0), stop=(n == HC - 1))
                    ins.then_inc(layer2_mm, 1)

            run_part2(pe, step2, experts, 4, RING + 2)


_INS = ['x', 'L0_tok_weights', 'L0_attn_Wk', 'L0_attn_bk', 'L0_attn_Wq', 'L0_attn_bq', 'L0_attn_Wv', 'L0_attn_bv',
        'L0_ffn_W1', 'L0_ffn_b1', 'L0_ffn_W2', 'L0_ffn_b2', 'L0_ffn_Wg', 'L0_ffn_bg']


def kernel(**inputs):
    import numpy as _np
    import concourse.bacc as _bacc
    from concourse import mybir as _mybir
    from concourse.bass_utils import run_bass_kernel_spmd as _run

    nc = _bacc.Bacc("TRN2", target_bir_lowering=False, num_devices=1)
    arrays, args = {}, []
    for name in _INS:
        a = _np.ascontiguousarray(inputs[name])
        arrays[f"in_{name}_dram"] = a
        args.append(nc.dram_tensor(f"in_{name}_dram", a.shape, _mybir.dt.from_np(a.dtype), kind="ExternalInput").ap())
    b, t, c = inputs['x'].shape
    taps = inputs['L0_tok_weights'].shape[2]
    args.append(nc.dram_tensor("out_0_dram", (b, t - taps + 1, c), _mybir.dt.float32, kind="ExternalOutput").ap())
    audio_tower(nc, *args)
    r = _run(nc, [arrays], core_ids=[0])
    return r.results[0]["out_0_dram"]
```

```python
from contextlib import ExitStack

import concourse.bass as bass
from concourse import mybir

FP32 = mybir.dt.float32
BF16 = mybir.dt.bfloat16
INT32 = mybir.dt.int32
UINT32 = mybir.dt.uint32
ALU = mybir.AluOpType
ACT = mybir.ActivationFunctionType
AX = mybir.AxisListType

MASKED = -1.0e30
EPS = 1e-5


class Turn:

    def __init__(self, loop, times, offset):
        self.loop, self.times, self.offset = loop, times, offset

    def __add__(self, n):
        return Turn(self.loop, self.times, self.offset + n)

    def of(self, n):
        return self.offset % n

    def count(self, per, extra=0):
        return self.loop * (self.times * per) + (self.offset * per + extra)

    def uses(self, n, per, extra=0):
        return self.loop * (self.times // n * per) + (self.offset // n * per + extra)

    def at_least(self, n):
        return not isinstance(self.loop, int) or self.offset >= n


def audio_tower(nc, x, tok_w, wk, bk, wq, bq, wv, bv, w1, b1, w2, b2, wg, bg, out):
    B, TX, D = x.shape
    TAPS = tok_w.shape[2]
    L = TX - TAPS + 1
    E, _, H = w1.shape
    N = B * L
    PER = 2
    GROUPS = B // PER
    HALF = L // 2
    TILES = 2 * PER
    GT = PER * L
    HC = H // 128
    REGION = -(-N // 128) * 128 + 128
    PADDING = E * REGION
    ROW = D + 3
    SHIFT, RSTD, TOKEN = D, D + 1, D + 2
    SLOTS = (N + E * 127) // 128
    EARLY = 24
    EARLY_GROUPS = GROUPS - 3
    assert (EARLY_GROUPS * GT - E * 127) // 128 >= EARLY
    TABLE = -(-SLOTS // 8) * 8
    LATE = TABLE - EARLY
    assert EARLY <= LATE
    NOWHERE = 1 << 20
    READ_SCALE = float(D) ** -0.5
    BANKS = 3
    RING = 8
    OUTS = 8

    x_rows = x.rearrange("b t c -> (b t) c")
    out_rows = out.rearrange("b t c -> (b t) c")
    routed = nc.dram_tensor("routed", (PADDING + 128, ROW), FP32).ap()

    ctx = ExitStack()
    with ctx:
        def sb(name, shape, dt=FP32):
            return ctx.enter_context(nc.sbuf_tensor(name, shape, dt))

        def pb(name):
            return ctx.enter_context(nc.psum_tensor(name, [128, 512], FP32))

        def sem(name):
            return ctx.enter_context(nc.semaphore(name))

        ident = sb("ident", [128, 128])
        ident_bf = sb("ident_bf", [128, 128], BF16)
        mask_bf = sb("mask_bf", [128, HALF], BF16)
        before_bf = sb("before_bf", [128, HALF], BF16)
        ones_bf = sb("ones_bf", [128, 128], BF16)
        tokw_raw = sb("tokw_raw", [128, D * TAPS])
        tokw = sb("tokw", [128, TAPS, D])
        wq_s = sb("wq_s", [128, D])
        wk_s = sb("wk_s", [128, D])
        wv_s = sb("wv_s", [128, D])
        bq_s = sb("bq_s", [128, 1])
        bk_s = sb("bk_s", [128, 1])
        bv_s = sb("bv_s", [128, D])
        wg_s = sb("wg_s", [128, E])
        bg_s = sb("bg_s", [128, E])
        w1_s = sb("w1_s", [128, E, H])
        w2_s = sb("w2_s", [128, E, HC, D])
        b1_s = sb("b1_s", [128, E, H])
        b2_s = sb("b2_s", [128, E, D])
        eps_s = sb("eps_s", [128, TILES])
        power_s = sb("power_s", [128, TILES])
        zero_s = sb("zero_s", [128, TILES])
        ramp = sb("ramp", [128, E])
        zero_u = sb("zero_u", [128, TILES], UINT32)
        next_token = sb("next_token", [128, TILES], UINT32)
        group_step = sb("group_step", [128, TILES], UINT32)
        base = sb("base", [128, E])
        padding_rows = sb("padding_rows", [128, ROW])

        x_in = sb("x_in", [128, 2, 4, 128])
        xT = sb("xT", [128, 2, PER, TX])
        prod = sb("prod", [128, 2, TAPS, GT])
        hT = sb("hT", [128, 2, TILES, HALF])
        stats1 = sb("stats1", [128, TILES, 6])
        norm1 = sb("norm1", [128, 2, TILES, 2])
        m = sb("m", [128, 2, TILES, 128])
        hm = sb("hm", [128, 2, TILES, 128])
        mT = sb("mT", [128, 2, TILES, HALF])
        qT = sb("qT", [128, 2, PER, L])
        kT = sb("kT", [128, 2, PER, L])
        vb = sb("vb", [128, 2, TILES, 128])
        vs = sb("vs", [128, 2, TILES, 128])
        neg_max = sb("neg_max", [128, 2, TILES])
        den = sb("den", [128, 2, TILES])
        rden = sb("rden", [128, 2, TILES])
        probs = sb("probs", [128, 2, PER, L + HALF])
        rows = sb("rows", [128, 2, TILES, ROW])
        stats2 = sb("stats2", [128, TILES, 6])
        xf = sb("xf", [128, 2, TILES, 128])
        xfT = sb("xfT", [128, 2, TILES, HALF])
        logits = sb("logits", [128, TILES, E])
        top = sb("top", [128, TILES])
        is_top = sb("is_top", [128, TILES, E])
        top_ramp = sb("top_ramp", [128, TILES, E])
        first = sb("first", [128, TILES])
        onehot = sb("onehot", [128, 2, TILES + 1, E], BF16)
        place = sb("place", [128, TILES, E])
        place1 = sb("place1", [128, TILES, E])
        row_sum = sb("row_sum", [128, TILES])
        row_at = sb("row_at", [128, 2, TILES], UINT32)

        region_at = sb("region_at", [LATE, E])
        region_up = sb("region_up", [LATE, E])
        region_size = sb("region_size", [LATE, E])
        unit_s = sb("unit_s", [LATE, E + 1])
        row_end = sb("row_end", [1, E], INT32)
        held_up = sb("held_up", [LATE, E], INT32)
        tiles_i = sb("tiles_i", [LATE, E], INT32)
        tiles_f = sb("tiles_f", [LATE, E])
        ones_e = sb("ones_e", [LATE, E])
        tile_end = sb("tile_end", [LATE, 2, E])
        early_end = sb("early_end", [LATE, E + 1])
        taken = sb("taken", [LATE, E + 1])
        taken_rows = sb("taken_rows", [LATE, E + 1])
        skip_taken = sb("skip_taken", [LATE, E])
        late_skip = sb("late_skip", [LATE, E])
        skip = sb("skip", [LATE, E])
        slot_no = sb("slot_no", [LATE, E])
        ended = sb("ended", [LATE, E])
        skipped = sb("skipped", [LATE, E + 1])
        slot_at = sb("slot_at", [LATE, 2])
        table = sb("table", [1, 2, TABLE], INT32)

        tl = sb("tl", [128, RING, ROW])
        xs = sb("xs", [128, 2, 128])
        xsT = sb("xsT", [128, 2, 128])
        hid = sb("hid", [128, 2, H])
        hidT = sb("hidT", [128, 2, H])
        res = sb("res", [128, RING, D])
        token_at = sb("token_at", [128, RING], UINT32)
        done_rows = sb("done_rows", [128, OUTS, 128])

        conv_bank = [pb(f"conv_bank{i}") for i in range(BANKS)]
        turn_bank = pb("turn_bank")
        h_bank = pb("h_bank")
        k_bank = pb("k_bank")
        q_bank = pb("q_bank")
        read_bank = pb("read_bank")
        score_bank = [q_bank, k_bank]
        gate_out = turn_bank[0:HALF, 0:TILES * E].rearrange("p (j e) -> p j e", e=E)
        rank_out = turn_bank[0:HALF, 64:64 + (TILES + 1) * E].rearrange("p (j e) -> p j e", e=E)
        table_out = [bank[0:1, 0:2 * TABLE].rearrange("p (r n) -> p r n", r=2) for bank in (conv_bank[0], q_bank)]

        slot_banks = conv_bank + [h_bank, q_bank, k_bank, read_bank, turn_bank]

        def tiles_of(bank, n=TILES):
            return bank[0:HALF, 0:n * 128].rearrange("p (j c) -> p j c", c=128)

        taps_in = sem("taps_in")
        weights_in = sem("weights_in")
        values_scaled = sem("values_scaled")
        late_in = sem("late_in")
        ident_ready = sem("ident_ready")
        consts_made = sem("consts_made")
        const_steps = sem("const_steps")
        tokw_turned = sem("tokw_turned")
        tokw_ready = sem("tokw_ready")
        x_loaded = [sem(f"x_loaded{i}") for i in range(2)]
        x_turned = sem("x_turned")
        xT_ready = sem("xT_ready")
        conv_mm = sem("conv_mm")
        conv_tanh = sem("conv_tanh")
        conv_mul = sem("conv_mul")
        pool_sum = sem("pool_sum")
        vector_sum = sem("vector_sum")
        h_ready = sem("h_ready")
        h_turned = sem("h_turned")
        stats1_ready = sem("stats1_ready")
        moments1_ready = sem("moments1_ready")
        norm1_steps = sem("norm1_steps")
        rstd1_ready = sem("rstd1_ready")
        m_ready = sem("m_ready")
        hm_ready = sem("hm_ready")
        m_turned = sem("m_turned")
        mT_ready = sem("mT_ready")
        q_mm = sem("q_mm")
        k_mm = sem("k_mm")
        v_mm = sem("v_mm")
        q_ready = sem("q_ready")
        k_ready = sem("k_ready")
        v_ready = sem("v_ready")
        scores_mm = [sem(f"scores_mm{b}") for b in range(PER)]
        max_ready = [sem(f"max_ready{b}") for b in range(PER)]
        probs_ready = [sem(f"probs_ready{b}") for b in range(PER)]
        rden_ready = sem("rden_ready")
        vs_ready = sem("vs_ready")
        read_mm = sem("read_mm")
        h2_ready = sem("h2_ready")
        stats2_ready = sem("stats2_ready")
        moments2_ready = sem("moments2_ready")
        norm2_steps = sem("norm2_steps")
        rstd2_ready = sem("rstd2_ready")
        xf_ready = sem("xf_ready")
        xf_turned = sem("xf_turned")
        xfT_ready = sem("xfT_ready")
        gate_mm = sem("gate_mm")
        choice_steps = sem("choice_steps")
        onehot_ready = sem("onehot_ready")
        rank_mm = sem("rank_mm")
        place_steps = sem("place_steps")
        base_ready = sem("base_ready")
        place_ready = sem("place_ready")
        token_written = sem("token_written")
        token_next = sem("token_next")
        routed_out = [sem(f"routed_out{i}") for i in range(2)]
        padding_made = sem("padding_made")
        padding_out = sem("padding_out")
        table_steps = sem("table_steps")
        TABLE_STEPS = (8, 17)
        table_turned = sem("table_turned")
        taken_steps = sem("taken_steps")
        ends_ready = sem("ends_ready")
        table_ready = sem("table_ready")
        slot_loaded = [sem(f"slot_loaded{i}") for i in range(RING)]
        xs_ready = sem("xs_ready")
        token_at_ready = sem("token_at_ready")
        xs_turned = sem("xs_turned")
        xsT_ready = sem("xsT_ready")
        layer1_mm = sem("layer1_mm")
        hid_ready = sem("hid_ready")
        hid_turned = sem("hid_turned")
        hidT_ready = sem("hidT_ready")
        layer2_mm = sem("layer2_mm")
        done_ready = sem("done_ready")
        done_out = [sem(f"done_out{i}") for i in range(OUTS)]

        WARM_UP = 12
        CONSTS = 21

        block = ctx.enter_context(nc.Block())

        LAST_LAG = 4
        STEPS = GROUPS + LAST_LAG
        PEELED = 6

        def run_part1(eng, step):
            for s in range(PEELED):
                step(Turn(0, 2, s), s)
            loops = (GROUPS - PEELED) // 2
            with eng.Fori(0, loops) as i:
                for c in range(2):
                    step(Turn(i, 2, PEELED + c), None)
            for s in range(PEELED + 2 * loops, STEPS):
                step(Turn(0, 2, s), s)

        def in_groups(s, lag):
            return s is None or lag <= s < GROUPS + lag

        LAST_LAG2 = 5
        STEPS2 = SLOTS + LAST_LAG2
        PEELED2 = EARLY

        def slot_bank(j):
            beside = isinstance(j.loop, int) and j.offset < BESIDE
            return slot_banks[j.of(4)] if beside else slot_banks[j.of(8)]

        def run_part2(eng, step, experts=None, first=0, n=0):
            loops = (SLOTS - PEELED2) // RING
            with eng.Fori(0, loops) as i:
                if experts:
                    experts.load(Turn(i, RING, PEELED2 + -first), n)
                for c in range(RING):
                    step(Turn(i, RING, PEELED2 + c), None)
            for s in range(PEELED2 + RING * loops, STEPS2):
                step(Turn(0, RING, s), s)

        AT = (1, 1, 1, 1, 3, 3, 2, 2, 2)
        BESIDE = 20
        assert sum(AT) <= BESIDE

        def slot_steps(step2):
            begun = [0]

            def do(n):
                for _ in range(n):
                    step2(Turn(0, RING, begun[0]), begun[0])
                    begun[0] += 1

            return (lambda point: do(AT[point])), (lambda: do(PEELED2 - begun[0]))

        def in_slots(s, lag):
            return s is None or lag <= s < SLOTS + lag

        class Column:

            def __init__(self, eng, row, max_val, n=8):
                self.eng, self.row, self.max_val, self.n = eng, row, max_val, n
                self.known = {}
                self.loads = 0

            def load(self, first, n):
                regs = [self.eng.alloc_register(f"row{self.row}_{self.loads}_{i}") for i in range(n)]
                self.loads += 1
                at = first.count(1)
                self.eng.load(regs, table[0:1, self.row, slice(at, at + n) if isinstance(at, int) else bass.ds(at, n)])
                for i, reg in enumerate(regs):
                    self.known[id(first.loop), first.offset + i] = self.eng.snap(reg, donate=True, min_val=0,
                                                                                max_val=self.max_val)

            def of(self, j):
                key = (id(j.loop), j.offset)
                if key not in self.known:
                    self.load(Turn(0, RING, j.offset // self.n * self.n), self.n)
                return self.known[key]

        @block.sync
        def _(sp):
            sp.dma_start(tokw_raw[:, :], tok_w.rearrange("d c k -> d (c k)")).then_inc(taps_in, 16)
            for g in range(2):
                sp.dma_start(x_in[:, g], x_rows[g * PER * TX:(g + 1) * PER * TX, :]
                             .rearrange("(j p) c -> p j c", p=128)).then_inc(x_loaded[g], 16)
            for dst, src in ((wq_s, wq), (wk_s, wk), (wv_s, wv), (wg_s, wg)):
                sp.dma_start(dst[:, :], src).then_inc(weights_in, 16)
            for dst, src in ((bq_s, bq), (bk_s, bk)):
                sp.dma_start(dst[:, :], src.rearrange("(p a) -> p a", a=1)).then_inc(weights_in, 16)
            sp.dma_start(bv_s[:, :], bv.rearrange("(a n) -> a n", a=1).to_broadcast((128, D))).then_inc(weights_in, 16)
            sp.dma_start(bg_s[:, :], bg.rearrange("(a n) -> a n", a=1).to_broadcast((128, E))).then_inc(weights_in, 16)
            sp.dma_start(w1_s[:, :, :], w1.rearrange("e d h -> d e h")).then_inc(late_in, 16)
            for n in range(HC):
                sp.dma_start(w2_s[:, :, n, :], w2[:, n * 128:(n + 1) * 128, :].rearrange("e p d -> p e d"))\
                  .then_inc(late_in, 16)
            sp.dma_start(b1_s[:, :, :].rearrange("p e h -> p (e h)"),
                         b1.rearrange("(a e) h -> a (e h)", a=1).to_broadcast((128, E * H))).then_inc(late_in, 16)
            sp.dma_start(b2_s[:, :, :], b2.unsqueeze(0).to_broadcast((128, E, D))).then_inc(late_in, 16)
            sp.wait_ge(padding_made, 2)
            sp.dma_start(routed[PADDING:PADDING + 128, :], padding_rows[:, :]).then_inc(padding_out, 16)

            def load_x(g):
                sp.wait_ge(x_turned, g.count(1, -1))
                sp.dma_start(x_in[:, g.of(2)], x_rows[bass.ds(g.count(PER * TX), PER * TX), :]
                             .rearrange("(j p) c -> p j c", p=128)).then_inc(x_loaded[g.of(2)], 16)

            with sp.Fori(1, GROUPS // 2) as i:
                for c in range(2):
                    load_x(Turn(i, 2, c))


            rows_at = Column(sp, 0, PADDING)

            def load_slot(j):
                if j.at_least(RING):
                    sp.wait_ge(token_at_ready, j.count(1, 1 - RING))
                at = rows_at.of(j)
                sp.dma_start(tl[:, j.of(RING)], routed[bass.ds(at, 128), :]).then_inc(slot_loaded[j.of(RING)], 16)

            sp.wait_ge(table_ready, 1)
            for n in range(2):
                sp.wait_ge(routed_out[n], 16 * TILES * len(range(n, EARLY_GROUPS, 2)))
            for j in range(EARLY - 4):
                load_slot(Turn(0, RING, j))

            sp.wait_ge(ends_ready, 1)
            ends = [sp.alloc_register(f"end{e}") for e in range(E)]
            sp.load(ends, row_end[0:1, 0:E])
            for e in range(E):
                end = sp.snap(ends[e], donate=True, min_val=e * REGION, max_val=e * REGION + N)
                sp.dma_start(routed[bass.ds(end, 128), :], padding_rows[:, :]).then_inc(padding_out, 16)
            for j in range(EARLY - 4, EARLY):
                load_slot(Turn(0, RING, j))

            sp.wait_ge(table_ready, 2)
            sp.wait_ge(padding_out, 16 * (E + 1))
            for n in range(2):
                sp.wait_ge(routed_out[n], 16 * TILES * GROUPS // 2)
            with sp.Fori(EARLY // RING, SLOTS // RING) as i:
                rows_at.load(Turn(i, RING, 0), RING)
                for c in range(RING):
                    load_slot(Turn(i, RING, c))
            for j in range(SLOTS // RING * RING, SLOTS):
                load_slot(Turn(0, RING, j))

        @block.gpsimd
        def _(pool):
            pool.memset(ident[:, :], 0.0).then_inc(const_steps, 1)
            pool.wait_ge(const_steps, 1)
            pool.affine_select(out=ident[:, :], in_=ident[:, :], compare_op=ALU.not_equal, fill=1.0, base=0,
                               pattern=[[-1, 128]], channel_multiplier=1).then_inc(ident_ready, 1)
            pool.memset(mask_bf[:, :], 0.0).then_inc(const_steps, 1)
            pool.memset(before_bf[:, :], 1.0).then_inc(const_steps, 1)
            pool.memset(padding_rows[:, 0:TOKEN], 0.0).then_inc(padding_made, 1)
            pool.memset(padding_rows[:, TOKEN:ROW].bitcast(UINT32), NOWHERE).then_inc(padding_made, 1)
            pool.memset(ones_bf[:, :], 1.0).then_inc(consts_made, 1)
            pool.memset(onehot[:, :, TILES, :], 0.0).then_inc(consts_made, 1)
            pool.memset(eps_s[:, :], EPS).then_inc(consts_made, 1)
            pool.memset(power_s[:, :], -0.5).then_inc(consts_made, 1)
            pool.memset(zero_s[:, :], 0.0).then_inc(consts_made, 1)
            pool.memset(zero_u[:, :], 0).then_inc(consts_made, 1)
            pool.memset(group_step[:, :], GT).then_inc(consts_made, 1)
            pool.memset(ones_e[:, :], 1.0).then_inc(consts_made, 1)
            pool.memset(region_size[:, :], float(REGION)).then_inc(consts_made, 1)
            pool.memset(unit_s[:, :], 128.0).then_inc(consts_made, 1)
            pool.memset(early_end[:, 0:1], 0.0).then_inc(consts_made, 1)
            pool.memset(taken[:, E:E + 1], 0.0).then_inc(consts_made, 1)
            pool.iota(ramp[:, :], [[-1, E]], base=E, channel_multiplier=0,
                      allow_small_or_imprecise_dtypes=True).then_inc(consts_made, 1)
            pool.iota(next_token[:, :], [[HALF, TILES]], base=0, channel_multiplier=1).then_inc(consts_made, 1)
            pool.iota(base[:, :], [[REGION, E]], base=0, channel_multiplier=0,
                      allow_small_or_imprecise_dtypes=True).then_inc(consts_made, 1)
            pool.iota(region_at[:, :], [[REGION, E]], base=0, channel_multiplier=0,
                      allow_small_or_imprecise_dtypes=True).then_inc(consts_made, 1)
            pool.iota(region_up[:, :], [[REGION, E]], base=-127, channel_multiplier=0,
                      allow_small_or_imprecise_dtypes=True).then_inc(consts_made, 1)
            pool.iota(slot_no[:, :], [[0, E]], base=0, channel_multiplier=1,
                      allow_small_or_imprecise_dtypes=True).then_inc(consts_made, 1)
            pool.iota(skipped[:, E:E + 1], [[0, 1]], base=0, channel_multiplier=128,
                      allow_small_or_imprecise_dtypes=True).then_inc(consts_made, 1)
            pool.wait_ge(const_steps, 3)
            pool.affine_select(out=mask_bf[:, :], in_=mask_bf[:, :], compare_op=ALU.is_ge, fill=MASKED, base=0,
                               pattern=[[1, HALF]], channel_multiplier=-1).then_inc(consts_made, 1)
            pool.affine_select(out=before_bf[:, :], in_=before_bf[:, :], compare_op=ALU.is_gt, fill=0.0, base=0,
                               pattern=[[1, HALF]], channel_multiplier=-1).then_inc(consts_made, 1)
            pool.wait_ge(consts_made, CONSTS)

            def normal(mean, var, moments_ready, steps, rstd_ready, g):
                pool.wait_ge(moments_ready, g.count(1, 1))
                pool.tensor_tensor(var, var, eps_s[0:HALF, :], ALU.add).then_inc(steps, 1)
                pool.tensor_tensor(mean, zero_s[0:HALF, :], mean, ALU.subtract).then_inc(steps, 1)
                pool.wait_ge(steps, g.count(3, 1))
                pool.tensor_tensor(var, var, power_s[0:HALF, :], ALU.pow).then_inc(steps, 1)
                pool.wait_ge(steps, g.count(3, 3))
                pool.tensor_tensor(mean, mean, var, ALU.mult).then_inc(rstd_ready, 1)

            def norm_h(g):
                normal(norm1[0:HALF, g.of(2), :, 0], norm1[0:HALF, g.of(2), :, 1], moments1_ready, norm1_steps,
                       rstd1_ready, g)

            def norm_h2(g):
                normal(rows[0:HALF, g.of(2), :, SHIFT], rows[0:HALF, g.of(2), :, RSTD], moments2_ready, norm2_steps,
                       rstd2_ready, g)

            def sum_tap(g, k):
                pool.wait_ge(conv_mul, g.count(TAPS, k + 1))
                if k > 1:
                    pool.wait_ge(pool_sum, g.count(3, k - 1))
                pool.tensor_tensor(prod[:, g.of(2), 0], prod[:, g.of(2), 0], prod[:, g.of(2), k], ALU.add)\
                    .then_inc(pool_sum, 1)

            def route(g):
                if g.at_least(2):
                    pool.wait_ge(routed_out[g.of(2)], g.uses(2, 16 * TILES))
                if g.at_least(1):
                    pool.wait_ge(token_next, g.count(1))
                pool.tensor_tensor(rows[0:HALF, g.of(2), :, TOKEN].bitcast(UINT32), next_token[0:HALF, :],
                                   zero_u[0:HALF, :], ALU.add).then_inc(token_written, 1)
                pool.wait_ge(token_written, g.count(1, 1))
                pool.wait_ge(place_ready, g.count(1, 1))
                pool.tensor_tensor(next_token[:, :], next_token[:, :], group_step[:, :], ALU.add)\
                    .then_inc(token_next, 1)
                for j in range(TILES):
                    pool.indirect_dma_start(
                        out=routed, out_offset=bass.IndirectOffsetOnAxis(ap=row_at[0:HALF, g.of(2), j:j + 1], axis=0),
                        in_=rows[0:HALF, g.of(2), j, :], in_offset=None).then_inc(routed_out[g.of(2)], 16)

            def taken_slots():
                pool.wait_ge(table_ready, 1)
                pool.tensor_tensor(taken[:, 0:E], early_end[:, 1:], early_end[:, 0:E], ALU.subtract)\
                    .then_inc(taken_steps, 1)
                pool.wait_ge(taken_steps, 1)
                pool.tensor_tensor(taken_rows[:, :], taken[:, :], unit_s[:, :], ALU.mult).then_inc(taken_steps, 1)
                pool.wait_ge(taken_steps, 2)
                pool.tensor_tensor(skip_taken[:, :], taken_rows[:, 1:], taken_rows[:, 0:E], ALU.subtract)\
                    .then_inc(taken_steps, 1)
                pool.tensor_tensor(skipped[:, E:E + 1], skipped[:, E:E + 1], taken_rows[:, 0:1], ALU.add)\
                    .then_inc(taken_steps, 1)
                pool.wait_ge(taken_steps, 4)
                pool.tensor_tensor(late_skip[:, :], skip_taken[:, :], region_size[:, :], ALU.add)\
                    .then_inc(taken_steps, 1)

            def step2(t, s):
                if in_slots(s, 5):
                    pool.wait_ge(done_ready, t.count(1, -4))
                    pool.wait_ge(token_at_ready, t.count(1, -4))
                if in_slots(s, 4):
                    j = t + -4
                    if j.at_least(RING):
                        pool.wait_ge(done_out[j.of(OUTS)], j.uses(OUTS, 16))
                    if s == 4:
                        pool.wait_ge(hid_ready, 1)
                    pool.tensor_tensor(token_at[:, j.of(RING):j.of(RING) + 1],
                                       tl[:, j.of(RING), TOKEN:ROW].bitcast(UINT32),
                                       zero_u[:, 0:1], ALU.add).then_inc(token_at_ready, 1)
                if in_slots(s, 5):
                    j = t + -5
                    pool.indirect_dma_start(
                        out=out_rows,
                        out_offset=bass.IndirectOffsetOnAxis(ap=token_at[:, j.of(RING):j.of(RING) + 1], axis=0),
                        in_=done_rows[:, j.of(OUTS)], in_offset=None,
                        bounds_check=N - 1, oob_is_err=False).then_inc(done_out[j.of(OUTS)], 16)

            slots_at, first_slots = slot_steps(step2)

            def step(t, s):
                if in_groups(s, 1):
                    norm_h(t + -1)
                if in_groups(s, 0):
                    sum_tap(t, 1)
                    sum_tap(t, 2)
                    sum_tap(t, 3)
                if s == GROUPS + 1:
                    taken_slots()
                    for point in range(4):
                        slots_at(point)
                if in_groups(s, 2):
                    norm_h2(t + -2)
                if s == GROUPS + 1:
                    slots_at(4)
                if s == GROUPS + 2:
                    for point in range(5, 8):
                        slots_at(point)
                if in_groups(s, 3):
                    route(t + -3)

            run_part1(pool, step)
            first_slots()

            run_part2(pool, step2)
            for n in range(OUTS):
                pool.wait_ge(done_out[n], 16 * len(range(n, SLOTS, OUTS)))

        @block.scalar
        def _(act):
            for n in range(2):
                act.wait_ge(tokw_turned, n + 1)
                src = conv_bank[n][:, :].rearrange("p (k d) -> p k d", d=D)
                take = min(4, TAPS - 4 * n)
                act.activation(tokw[:, 4 * n:4 * n + take, :], src[:, 0:take, :], ACT.Copy).then_inc(tokw_ready, 1)

            def copy_xT(g):
                act.wait_ge(x_turned, g.count(1, 1))
                if g.at_least(2):
                    act.wait_ge(conv_mul, g.count(TAPS, -TAPS))
                act.activation(xT[:, g.of(2)].rearrange("p b t -> p (b t)"), turn_bank[:, :], ACT.Copy)\
                    .then_inc(xT_ready, 1)

            def tanh(g, k):
                act.wait_ge(conv_mm, g.count(TAPS, k + 1))
                bank = conv_bank[(k + g.of(2)) % BANKS][:, 0:GT]
                act.activation(bank, bank, ACT.Tanh).then_inc(conv_tanh, 1)

            def normalize_h(g):
                act.wait_ge(rstd1_ready, g.count(1, 1))
                if g.at_least(2):
                    act.wait_ge(hm_ready, g.count(1, -1))
                    act.wait_ge(m_turned, g.count(1, -1))
                for j in range(TILES):
                    ins = act.activation(m[0:HALF, g.of(2), j, :], tiles_of(h_bank)[:, j, :], ACT.Identity,
                                         bias=norm1[0:HALF, g.of(2), j, 0:1], scale=norm1[0:HALF, g.of(2), j, 1:2])
                ins.then_inc(m_ready, 1)

            def copy_mT(g):
                act.wait_ge(m_turned, g.count(1, 1))
                if g.at_least(2):
                    act.wait_ge(q_mm, g.count(1, -1))
                    act.wait_ge(k_mm, g.count(1, -1))
                    act.wait_ge(v_mm, g.count(1, -1))
                act.activation(mT[:, g.of(2)].rearrange("p j t -> p (j t)"), h_bank[:, 0:GT], ACT.Copy)\
                    .then_inc(mT_ready, 1)

            def add_bias(dst, bank, bias, mm, ready, g):
                act.wait_ge(mm, g.count(1, 1))
                if g.at_least(2):
                    for b in range(PER):
                        act.wait_ge(scores_mm[b], g.count(1, -1))
                act.activation(dst[:, g.of(2)].rearrange("p b t -> p (b t)"), bank[:, 0:GT], ACT.Identity,
                               bias=bias[:, 0:1]).then_inc(ready, 1)

            def add_bq(g):
                add_bias(qT, q_bank, bq_s, q_mm, q_ready, g)

            def add_bk(g):
                add_bias(kT, k_bank, bk_s, k_mm, k_ready, g)

            def exps(g, b):
                act.wait_ge(max_ready[b], g.count(1, 1))
                if g.at_least(2):
                    act.wait_ge(read_mm, g.count(1, -1))
                    act.wait_ge(rden_ready, g.count(1, -1))
                for n, (lo, hi) in enumerate(((0, L), (L, L + HALF))):
                    n += 2 * b
                    ins = act.activation(probs[0:HALF, g.of(2), b, lo:hi], score_bank[b][0:HALF, lo:hi], ACT.Exp,
                                         bias=neg_max[0:HALF, g.of(2), n:n + 1],
                                         accum_out=den[0:HALF, g.of(2), n:n + 1])
                ins.then_inc(probs_ready[b], 1)

            def scale_values(g):
                act.wait_ge(rden_ready, g.count(1, 1))
                act.wait_ge(v_ready, g.count(1, 1))
                if g.at_least(2):
                    act.wait_ge(read_mm, g.count(1, -1))
                for j in range(TILES):
                    ins = act.activation(vs[0:HALF, g.of(2), j, :], vb[0:HALF, g.of(2), j, :], ACT.Copy,
                                         scale=rden[0:HALF, g.of(2), j:j + 1])
                ins.then_inc(vs_ready, 1)

            def normalize_h2(g):
                act.wait_ge(rstd2_ready, g.count(1, 1))
                if g.at_least(2):
                    act.wait_ge(xf_turned, g.count(1, -1))
                rr = rows[0:HALF, g.of(2)]
                for j in range(TILES):
                    ins = act.activation(xf[0:HALF, g.of(2), j, :], rr[:, j, 0:D], ACT.Identity,
                                         bias=rr[:, j, SHIFT:SHIFT + 1], scale=rr[:, j, RSTD:RSTD + 1])
                ins.then_inc(xf_ready, 1)

            def copy_xfT(g):
                act.wait_ge(xf_turned, g.count(1, 1))
                if g.at_least(2):
                    act.wait_ge(gate_mm, g.count(1, -1))
                act.activation(xfT[:, g.of(2)].rearrange("p j t -> p (j t)"), turn_bank[:, 0:GT], ACT.Copy)\
                    .then_inc(xfT_ready, 1)

            def scale_values_weights():
                act.wait_ge(weights_in, 16 * 8)
                act.activation(wv_s[:, :], wv_s[:, :], ACT.Copy, scale=READ_SCALE).then_inc(values_scaled, 1)
                act.activation(bv_s[:, :], bv_s[:, :], ACT.Copy, scale=READ_SCALE).then_inc(values_scaled, 1)

            def step2(t, s):
                if in_slots(s, 1):
                    j = t + -1
                    act.wait_ge(xs_turned, j.count(1, 1))
                    act.activation(xsT[:, j.of(2)], slot_bank(j)[:, 0:D], ACT.Copy).then_inc(xsT_ready, 1)
                if in_slots(s, 0):
                    j = t
                    act.wait_ge(slot_loaded[j.of(RING)], j.uses(RING, 16, 16))
                    row = tl[:, j.of(RING)]
                    act.activation(xs[:, j.of(2)], row[:, 0:D], ACT.Identity, bias=row[:, SHIFT:SHIFT + 1],
                                   scale=row[:, RSTD:RSTD + 1]).then_inc(xs_ready, 1)
                if in_slots(s, 3):
                    j = t + -3
                    act.wait_ge(hid_turned, j.count(1, 1))
                    act.activation(hidT[:, j.of(2)], slot_bank(j)[:, 0:H], ACT.Relu).then_inc(hidT_ready, 1)

            slots_at, first_slots = slot_steps(step2)

            def step(t, s):
                if s == 1:
                    scale_values_weights()
                if in_groups(s, 0):
                    copy_xT(t)
                if in_groups(s, 2):
                    copy_mT(t + -2)
                if s == GROUPS + 1:
                    slots_at(0)
                if in_groups(s, 1):
                    tanh(t + -1, 6)
                if in_groups(s, 2):
                    add_bq(t + -2)
                if in_groups(s, 0):
                    tanh(t, 0)
                if in_groups(s, 2):
                    add_bk(t + -2)
                if s == GROUPS + 1:
                    slots_at(1)
                if in_groups(s, 0):
                    tanh(t, 1)
                if in_groups(s, 3):
                    normalize_h2(t + -3)
                if s == GROUPS + 2:
                    for point in range(5, 6):
                        slots_at(point)
                if in_groups(s, 0):
                    tanh(t, 2)
                if in_groups(s, 2):
                    exps(t + -2, 1)
                    exps(t + -2, 0)
                if in_groups(s, 3):
                    copy_xfT(t + -3)
                if in_groups(s, 2):
                    scale_values(t + -2)
                if s == GROUPS + 1:
                    for point in range(2, 5):
                        slots_at(point)
                if in_groups(s, 0):
                    tanh(t, 3)
                    tanh(t, 4)
                if in_groups(s, 1):
                    normalize_h(t + -1)
                if in_groups(s, 0):
                    tanh(t, 5)

            run_part1(act, step)
            for point in range(6, 9):
                slots_at(point)
            first_slots()

            run_part2(act, step2)

        @block.vector
        def _(dve):
            dve.wait_ge(consts_made, CONSTS)
            dve.wait_ge(ident_ready, 1)
            dve.tensor_copy(ident_bf[:, :], ident[:, :]).then_inc(consts_made, 1)

            def mul(g, k):
                dve.wait_ge(conv_tanh, g.count(TAPS, k + 1))
                if k == 0 and g.at_least(2):
                    dve.wait_ge(h_ready, g.count(1, -1))
                w = conv_bank[(k + g.of(2)) % BANKS][:, 0:GT].rearrange("p (b t) -> p b t", b=PER)
                dve.tensor_tensor(prod[:, g.of(2), k].rearrange("p (b t) -> p b t", b=PER), w,
                                  xT[:, g.of(2), :, k:k + L], ALU.mult).then_inc(conv_mul, 1)

            def add_tap5(g):
                dve.wait_ge(conv_mul, g.count(TAPS, 6))
                dve.tensor_tensor(prod[:, g.of(2), 4], prod[:, g.of(2), 4], prod[:, g.of(2), 5], ALU.add)\
                    .then_inc(vector_sum, 1)

            def add_tap6(g):
                dve.wait_ge(conv_mul, g.count(TAPS, 7))
                dve.wait_ge(vector_sum, g.count(2, 1))
                dve.tensor_tensor(prod[:, g.of(2), 4], prod[:, g.of(2), 4], prod[:, g.of(2), 6], ALU.add)\
                    .then_inc(vector_sum, 1)

            def add_h(g):
                dve.wait_ge(vector_sum, g.count(2, 2))
                dve.wait_ge(pool_sum, g.count(3, 3))
                if g.at_least(2):
                    dve.wait_ge(h_turned, g.count(1, -1))
                dve.tensor_tensor(hT[:, g.of(2)].rearrange("p j t -> p (j t)"), prod[:, g.of(2), 0],
                                  prod[:, g.of(2), 4], ALU.add).then_inc(h_ready, 1)

            def stats_h(g):
                dve.wait_ge(h_turned, g.count(1, 1))
                for j in range(TILES):
                    ins = dve.bn_stats(stats1[0:HALF, j, :], tiles_of(h_bank)[:, j, :])
                ins.then_inc(stats1_ready, 1)

            def moments_h(g):
                for j in range(TILES):
                    ins = dve.bn_aggr(norm1[0:HALF, g.of(2), j, :], stats1[0:HALF, j, :])
                ins.then_inc(moments1_ready, 1)

            def add_m(g):
                dve.wait_ge(m_ready, g.count(1, 1))
                if g.at_least(2):
                    dve.wait_ge(h2_ready, g.count(1, -1))
                dve.tensor_tensor(hm[0:HALF, g.of(2)], tiles_of(h_bank), m[0:HALF, g.of(2)], ALU.add)\
                    .then_inc(hm_ready, 1)

            def add_bv(g):
                dve.wait_ge(v_mm, g.count(1, 1))
                if g.at_least(2):
                    dve.wait_ge(vs_ready, g.count(1, -1))
                dve.tensor_tensor(vb[0:HALF, g.of(2)], tiles_of(read_bank),
                                  bv_s[0:HALF].unsqueeze(1).to_broadcast((HALF, TILES, D)), ALU.add)\
                    .then_inc(v_ready, 1)

            def maxima(g, b):
                dve.wait_ge(scores_mm[b], g.count(1, 1))
                if g.at_least(2):
                    dve.wait_ge(probs_ready[b], g.count(1, -1))
                for n, (lo, hi) in enumerate(((0, L), (L, L + HALF))):
                    n += 2 * b
                    ins = dve.tensor_reduce(neg_max[0:HALF, g.of(2), n:n + 1], score_bank[b][0:HALF, lo:hi],
                                            axis=AX.X, op=ALU.max, negate=True)
                ins.then_inc(max_ready[b], 1)

            def divide(g):
                for b in range(PER):
                    dve.wait_ge(probs_ready[b], g.count(1, 1))
                if g.at_least(2):
                    dve.wait_ge(vs_ready, g.count(1, -1))
                dve.reciprocal(rden[0:HALF, g.of(2)], den[0:HALF, g.of(2)]).then_inc(rden_ready, 1)

            def add_read(g):
                dve.wait_ge(read_mm, g.count(1, 1))
                dve.wait_ge(hm_ready, g.count(1, 1))
                if g.at_least(2):
                    dve.wait_ge(routed_out[g.of(2)], g.uses(2, 16 * TILES))
                dve.tensor_tensor(rows[0:HALF, g.of(2), :, 0:D], tiles_of(read_bank), hm[0:HALF, g.of(2)], ALU.add)\
                    .then_inc(h2_ready, 1)

            def stats_h2(g):
                dve.wait_ge(h2_ready, g.count(1, 1))
                for j in range(TILES):
                    ins = dve.bn_stats(stats2[0:HALF, j, :], rows[0:HALF, g.of(2), j, 0:D])
                ins.then_inc(stats2_ready, 1)

            def moments_h2(g):
                for j in range(TILES):
                    ins = dve.bn_aggr(rows[0:HALF, g.of(2), j, SHIFT:SHIFT + 2], stats2[0:HALF, j, :])
                ins.then_inc(moments2_ready, 1)

            def choose_logits(g):
                dve.wait_ge(gate_mm, g.count(1, 1))
                dve.tensor_tensor(logits[0:HALF], gate_out, bg_s[0:HALF].unsqueeze(1).to_broadcast((HALF, TILES, E)),
                                  ALU.add).then_inc(choice_steps, 1)

            def choose_top(g):
                dve.wait_ge(choice_steps, g.count(5, 1))
                dve.tensor_reduce(top[0:HALF], logits[0:HALF], axis=AX.X, op=ALU.max).then_inc(choice_steps, 1)

            def choose_is_top(g):
                dve.wait_ge(choice_steps, g.count(5, 2))
                dve.tensor_tensor(is_top[0:HALF], logits[0:HALF],
                                  top[0:HALF].unsqueeze(2).to_broadcast((HALF, TILES, E)), ALU.is_equal)\
                    .then_inc(choice_steps, 1)

            def choose_ramp(g):
                dve.wait_ge(choice_steps, g.count(5, 3))
                dve.tensor_tensor(top_ramp[0:HALF], is_top[0:HALF],
                                  ramp[0:HALF].unsqueeze(1).to_broadcast((HALF, TILES, E)), ALU.mult)\
                    .then_inc(choice_steps, 1)

            def choose_first(g):
                dve.wait_ge(choice_steps, g.count(5, 4))
                dve.tensor_reduce(first[0:HALF], top_ramp[0:HALF], axis=AX.X, op=ALU.max).then_inc(choice_steps, 1)

            def choose_one(g):
                dve.wait_ge(choice_steps, g.count(5, 5))
                if g.at_least(2):
                    dve.wait_ge(rank_mm, g.count(1, -1))
                dve.tensor_tensor(onehot[0:HALF, g.of(2), 0:TILES],
                                  ramp[0:HALF].unsqueeze(1).to_broadcast((HALF, TILES, E)),
                                  first[0:HALF].unsqueeze(2).to_broadcast((HALF, TILES, E)), ALU.is_equal)\
                    .then_inc(onehot_ready, 1)

            def place_ranks(g):
                dve.wait_ge(rank_mm, g.count(1, 1))
                if g.at_least(1):
                    dve.wait_ge(base_ready, g.count(1))
                dve.tensor_tensor(place[0:HALF], rank_out[:, 0:TILES],
                                  base[0:HALF].unsqueeze(1).to_broadcast((HALF, TILES, E)),
                                  ALU.add).then_inc(place_steps, 1)

            def place_own(g):
                dve.wait_ge(place_steps, g.count(3, 1))
                dve.tensor_tensor(base[0:HALF], base[0:HALF], rank_out[:, TILES], ALU.add).then_inc(base_ready, 1)
                dve.tensor_tensor(place1[0:HALF], place[0:HALF], onehot[0:HALF, g.of(2), 0:TILES], ALU.mult)\
                    .then_inc(place_steps, 1)

            def place_sum(g):
                dve.wait_ge(place_steps, g.count(3, 2))
                dve.tensor_reduce(row_sum[0:HALF], place1[0:HALF], axis=AX.X, op=ALU.add).then_inc(place_steps, 1)

            def place_rows(g):
                dve.wait_ge(place_steps, g.count(3, 3))
                if g.at_least(2):
                    dve.wait_ge(routed_out[g.of(2)], g.uses(2, 16 * TILES))
                dve.tensor_copy(row_at[0:HALF, g.of(2)], row_sum[0:HALF]).then_inc(place_ready, 1)

            done = [0]

            def then(ins):
                done[0] += 1
                ins.then_inc(table_steps, 1)
                dve.wait_ge(table_steps, done[0])

            def begin_table(late):
                dve.wait_ge(base_ready, GROUPS if late else EARLY_GROUPS)
                if late:
                    dve.tensor_copy(row_end[:, :], base[0:1, :]).then_inc(ends_ready, 1)
                then(dve.tensor_tensor(held_up[:, :], base[0:LATE, :], (region_up if late else region_at)[:, :],
                                       ALU.subtract))
                then(dve.tensor_single_scalar(tiles_i[:, :], held_up[:, :], 7, ALU.arith_shift_right))
                then(dve.tensor_copy(tiles_f[:, :], tiles_i[:, :]))
                if late:
                    dve.wait_ge(taken_steps, 5)
                    then(dve.tensor_tensor(tiles_f[:, :], tiles_f[:, :], taken[:, 0:E], ALU.subtract))
                then(dve.tensor_tensor_scan(tile_end[:, late], ones_e[:, :], tiles_f[:, :], 0.0, ALU.mult, ALU.add))
                then(dve.tensor_tensor(ended[:, :], slot_no[:, :], tile_end[:, late], ALU.is_ge))
                then(dve.scalar_tensor_tensor(skip[:, :], tiles_f[:, :], -128.0,
                                              (late_skip if late else region_size)[:, :], ALU.mult, ALU.add))
                then(dve.tensor_tensor(skipped[:, 0:E], ended[:, :], skip[:, :], ALU.mult))
                dve.tensor_reduce(slot_at[:, 0:1], skipped[:, :], axis=AX.X, op=ALU.add)
                then(dve.tensor_reduce(slot_at[:, 1:2], ended[:, :], axis=AX.X, op=ALU.add))
                assert done[0] == TABLE_STEPS[late]

            def end_table(late):
                lo, hi = (EARLY, TABLE) if late else (0, EARLY)
                dve.wait_ge(table_turned, 1 + late)
                if not late:
                    dve.tensor_scalar(early_end[:, 1:], tile_end[:, 0, :], float(EARLY), None, ALU.min)
                for row, most in ((0, PADDING), (1, E - 1)):
                    ins = dve.tensor_scalar(table[:, row, lo:hi], table_out[late][:, row, 0:hi - lo], float(most),
                                            None, ALU.min)
                ins.then_inc(table_ready, 1)

            experts = Column(dve, 1, E - 1)

            def step2(t, s):
                if in_slots(s, 5):
                    j = t + -5
                    dve.wait_ge(layer2_mm, j.count(1, 1))
                    if j.at_least(OUTS):
                        dve.wait_ge(done_out[j.of(OUTS)], j.uses(OUTS, 16))
                    dve.tensor_tensor(done_rows[:, j.of(OUTS)], slot_bank(j)[:, D + H:2 * D + H],
                                      res[:, j.of(RING)], ALU.add)\
                        .then_inc(done_ready, 1)
                if in_slots(s, 2):
                    j = t + -2
                    if s == 2:
                        dve.wait_ge(table_ready, 1)
                        dve.wait_ge(late_in, 16 * (3 + HC))
                    e = experts.of(j)
                    dve.wait_ge(layer1_mm, j.count(1, 1))
                    dve.tensor_tensor(res[:, j.of(RING)], tl[:, j.of(RING), 0:D],
                                      b2_s[:, bass.ds(e, 1), :].rearrange("p a d -> p (a d)"), ALU.add)
                    dve.tensor_tensor(hid[:, j.of(2)], slot_bank(j)[:, D:D + H],
                                      b1_s[:, bass.ds(e, 1), :].rearrange("p a h -> p (a h)"), ALU.add)\
                        .then_inc(hid_ready, 1)

            slots_at, first_slots = slot_steps(step2)

            def step(t, s):
                if in_groups(s, 3):
                    add_bv(t + -3)
                if in_groups(s, 2):
                    dve.wait_ge(stats1_ready, (t + -2).count(1, 1))
                if in_groups(s, 3):
                    divide(t + -3)
                if in_groups(s, 2):
                    moments_h(t + -2)
                if in_groups(s, 1):
                    mul(t + -1, 2)
                if s == GROUPS + 2:
                    slots_at(2)
                if s == GROUPS + 3:
                    slots_at(5)
                    slots_at(6)
                if in_groups(s, 4):
                    choose_logits(t + -4)
                    choose_top(t + -4)
                    choose_is_top(t + -4)
                    choose_ramp(t + -4)
                    choose_first(t + -4)
                    choose_one(t + -4)
                if s == GROUPS + 2:
                    slots_at(3)
                if s == GROUPS + 3:
                    slots_at(7)
                if in_groups(s, 1):
                    mul(t + -1, 3)
                    mul(t + -1, 4)
                if in_groups(s, 3):
                    add_read(t + -3)
                if in_groups(s, 2):
                    add_m(t + -2)
                if in_groups(s, 3):
                    stats_h2(t + -3)
                    dve.wait_ge(stats2_ready, (t + -3).count(1, 1))
                if in_groups(s, 1):
                    mul(t + -1, 5)
                if in_groups(s, 3):
                    moments_h2(t + -3)
                if in_groups(s, 1):
                    add_tap5(t + -1)
                    mul(t + -1, 6)
                if s == GROUPS + 1:
                    slots_at(0)
                if s == GROUPS + 2:
                    slots_at(4)
                if in_groups(s, 4):
                    place_ranks(t + -4)
                if s == GROUPS + 1:
                    slots_at(1)
                if in_groups(s, 1):
                    add_tap6(t + -1)
                if in_groups(s, 4):
                    place_own(t + -4)
                if in_groups(s, 0):
                    mul(t, 0)
                if in_groups(s, 4):
                    place_sum(t + -4)
                if in_groups(s, 1):
                    add_h(t + -1)
                if in_groups(s, 4):
                    place_rows(t + -4)
                if s == GROUPS:
                    begin_table(0)
                if in_groups(s, 0):
                    mul(t, 1)
                if in_groups(s, 2):
                    maxima(t + -2, 1)
                    maxima(t + -2, 0)
                if in_groups(s, 1):
                    stats_h(t + -1)
                if s == GROUPS:
                    end_table(0)

            run_part1(dve, step)
            begin_table(1)
            slots_at(8)
            end_table(1)
            dve.wait_ge(table_ready, 2)
            first_slots()

            run_part2(dve, step2, experts, 4, RING + 4)

        @block.tensor
        def _(pe):
            pe.wait_ge(ident_ready, 1)
            for _ in range(WARM_UP):
                pe.transpose(h_bank[:, 0:128], ident[:, :], ident[:, :])
            pe.wait_ge(taps_in, 16)
            raw = tokw_raw[:, :].rearrange("d (c k) -> d k c", k=TAPS)
            for k in range(TAPS):
                ins = pe.transpose(conv_bank[k // 4][:, k % 4 * 128:(k % 4 + 1) * 128], raw[:, k, :], ident[:, :])
                if k == 3 or k == TAPS - 1:
                    ins.then_inc(tokw_turned, 1)

            def bank_free(users, g):
                if not isinstance(g.loop, int):
                    taken, ahead = users[0]
                    pe.wait_ge(taken, g.count(1, ahead + 1))
                    return
                for taken, ahead in users:
                    if min(g.offset + ahead, GROUPS - 1) >= 0:
                        pe.wait_ge(taken, min(g.offset + ahead, GROUPS - 1) + 1)

            def turn_x(g):
                bank_free([(onehot_ready, -4), (xfT_ready, -4), (base_ready, -5), (xT_ready, -1)], g)
                pe.wait_ge(x_loaded[g.of(2)], g.uses(2, 16, 16))
                for j in range(4):
                    ins = pe.transpose(turn_bank[:, j * 128:(j + 1) * 128], x_in[:, g.of(2), j, :], ident[:, :])
                ins.then_inc(x_turned, 1)


            def conv(g, k):
                if k == 0:
                    pe.wait_ge(xT_ready, g.count(1, 1))
                n = (k + g.of(2)) % BANKS
                if k >= BANKS:
                    pe.wait_ge(conv_mul, g.count(TAPS, k - BANKS + 1))
                elif g.at_least(1):
                    last = max(q for q in range(TAPS) if (q + 1 - g.of(2)) % BANKS == n)
                    pe.wait_ge(conv_mul, g.count(TAPS, last + 1 - TAPS))
                pe.matmul(conv_bank[n][:, 0:GT], tokw[:, k, :], xT[:, g.of(2), :, TAPS - 1:TX],
                          start=True, stop=True).then_inc(conv_mm, 1)

            def turn_h(g):
                bank_free([(mT_ready, -1), (hm_ready, -1)], g)
                pe.wait_ge(h_ready, g.count(1, 1))
                for j in range(TILES):
                    ins = pe.transpose(tiles_of(h_bank)[:, j, :], hT[:, g.of(2), j, :], ident[:, :])
                ins.then_inc(h_turned, 1)

            def turn_m(g):
                bank_free([(hm_ready, 0), (mT_ready, -1)], g)
                pe.wait_ge(m_ready, g.count(1, 1))
                for j in range(TILES):
                    ins = pe.transpose(h_bank[:, j * HALF:(j + 1) * HALF], m[0:HALF, g.of(2), j, :],
                                       ident[0:HALF, 0:HALF])
                ins.then_inc(m_turned, 1)

            def queries(g):
                bank_free([(probs_ready[0], -1), (q_ready, -1)], g)
                pe.wait_ge(mT_ready, g.count(1, 1))
                pe.matmul(q_bank[:, 0:GT], wq_s[:, :], mT[:, g.of(2)].rearrange("p j t -> p (j t)"),
                          start=True, stop=True).then_inc(q_mm, 1)

            def keys(g):
                bank_free([(probs_ready[1], -1), (k_ready, -1)], g)
                pe.wait_ge(mT_ready, g.count(1, 1))
                pe.matmul(k_bank[:, 0:GT], wk_s[:, :], mT[:, g.of(2)].rearrange("p j t -> p (j t)"),
                          start=True, stop=True).then_inc(k_mm, 1)

            def values(g):
                bank_free([(h2_ready, -1), (v_ready, -1)], g)
                pe.wait_ge(mT_ready, g.count(1, 1))
                for j in range(TILES):
                    ins = pe.matmul(tiles_of(read_bank)[:, j, :], mT[:, g.of(2), j, :], wv_s[:, :],
                                    start=True, stop=True)
                ins.then_inc(v_mm, 1)

            def scores(g, b):
                bank_free([[(q_ready, 0), (probs_ready[0], -1)], [(k_ready, 0), (probs_ready[1], -1)]][b], g)
                pe.wait_ge(q_ready, g.count(1, 1))
                pe.wait_ge(k_ready, g.count(1, 1))
                for n, (lo, hi) in enumerate(((0, L), (L, L + HALF))):
                    pe.matmul(score_bank[b][0:HALF, lo:hi], kT[:, g.of(2), b, n * HALF:(n + 1) * HALF],
                              qT[:, g.of(2), b, n * HALF:L], start=True, stop=False)
                    ins = pe.matmul(score_bank[b][0:HALF, lo:lo + HALF], ident_bf[0:HALF, 0:HALF],
                                    mask_bf[0:HALF, :], start=False, stop=True)
                ins.then_inc(scores_mm[b], 1)

            def read(g):
                bank_free([(v_ready, 0), (h2_ready, -1)], g)
                for b in range(PER):
                    pe.wait_ge(probs_ready[b], g.count(1, 1))
                pe.wait_ge(vs_ready, g.count(1, 1))
                out = tiles_of(read_bank)
                for b in range(PER):
                    p = probs[0:HALF, g.of(2), b]
                    v0, v1 = vs[0:HALF, g.of(2), 2 * b, :], vs[0:HALF, g.of(2), 2 * b + 1, :]
                    pe.matmul(out[:, 2 * b, :], p[:, 0:HALF], v0, start=True, stop=True)
                    pe.matmul(out[:, 2 * b + 1, :], p[:, HALF:L], v0, start=True, stop=False)
                    ins = pe.matmul(out[:, 2 * b + 1, :], p[:, L:L + HALF], v1, start=False, stop=True)
                ins.then_inc(read_mm, 1)

            def turn_xf(g):
                bank_free([(base_ready, -1), (xT_ready, 3), (onehot_ready, -1), (xfT_ready, -1)], g)
                pe.wait_ge(xf_ready, g.count(1, 1))
                for j in range(TILES):
                    ins = pe.transpose(turn_bank[:, j * HALF:(j + 1) * HALF], xf[0:HALF, g.of(2), j, :],
                                       ident[0:HALF, 0:HALF])
                ins.then_inc(xf_turned, 1)

            def gate(g):
                bank_free([(xfT_ready, 0), (base_ready, -1), (xT_ready, 3), (onehot_ready, -1)], g)
                pe.wait_ge(xfT_ready, g.count(1, 1))
                for j in range(TILES):
                    ins = pe.matmul(gate_out[:, j, :], xfT[:, g.of(2), j, :], wg_s[:, :], start=True, stop=True)
                ins.then_inc(gate_mm, 1)

            def ranks(g):
                bank_free([(xT_ready, 4), (onehot_ready, 0), (xfT_ready, 0), (base_ready, -1)], g)
                pe.wait_ge(onehot_ready, g.count(1, 1))
                chosen = onehot[0:HALF, g.of(2)]
                pe.matmul(rank_out, before_bf[0:HALF, :], chosen, start=True, stop=False)
                for j in range(TILES):
                    n = TILES - j
                    ins = pe.matmul(rank_out[:, j + 1:], ones_bf[0:HALF, 0:HALF],
                                    chosen[:, j:j + 1, :].to_broadcast((HALF, n, E)), start=False, stop=(n == 1))
                ins.then_inc(rank_mm, 1)

            def turn_table(late):
                pe.wait_ge(table_steps, TABLE_STEPS[late])
                P = TABLE - EARLY if late else EARLY
                for n in range(2):
                    ins = pe.matmul(table_out[late][:, n, 0:P], slot_at[0:P, n:n + 1], ident[0:P, 0:P],
                                    start=True, stop=True)
                ins.then_inc(table_turned, 1)

            experts = Column(pe, 1, E - 1)

            def step2(t, s):
                if in_slots(s, 2):
                    j = t + -2
                    e = experts.of(j)
                    pe.wait_ge(xsT_ready, j.count(1, 1))
                    pe.matmul(slot_bank(j)[:, D:D + H], xsT[:, j.of(2)],
                              w1_s[:, bass.ds(e, 1), :].rearrange("p a h -> p (a h)"), start=True, stop=True)\
                        .then_inc(layer1_mm, 1)
                if in_slots(s, 1):
                    j = t + -1
                    if s == 1:
                        pe.wait_ge(table_ready, 1)
                        pe.wait_ge(late_in, 16 * (3 + HC))
                    pe.wait_ge(xs_ready, j.count(1, 1))
                    if isinstance(j.loop, int) and 4 <= j.offset < BESIDE:
                        pe.wait_ge(done_ready, j.offset - 3)
                    pe.transpose(slot_bank(j)[:, 0:D], xs[:, j.of(2)], ident[:, :]).then_inc(xs_turned, 1)
                if in_slots(s, 3):
                    j = t + -3
                    pe.wait_ge(hid_ready, j.count(1, 1))
                    for n in range(HC):
                        ins = pe.transpose(slot_bank(j)[:, n * 128:(n + 1) * 128],
                                           hid[:, j.of(2), n * 128:(n + 1) * 128], ident[:, :])
                    ins.then_inc(hid_turned, 1)
                if in_slots(s, 4):
                    j = t + -4
                    e = experts.of(j)
                    pe.wait_ge(hidT_ready, j.count(1, 1))
                    for n in range(HC):
                        ins = pe.matmul(slot_bank(j)[:, D + H:2 * D + H], hidT[:, j.of(2), n * 128:(n + 1) * 128],
                                        w2_s[:, bass.ds(e, 1), n, :].rearrange("p a d -> p (a d)"),
                                        start=(n == 0), stop=(n == HC - 1))
                    ins.then_inc(layer2_mm, 1)

            slots_at, first_slots = slot_steps(step2)

            def step(t, s):
                if s == 2:
                    pe.wait_ge(values_scaled, 2)
                    pe.wait_ge(consts_made, CONSTS + 1)
                if s == GROUPS + 3:
                    slots_at(6)
                if in_groups(s, 4):
                    gate(t + -4)
                if s == GROUPS + 2:
                    slots_at(3)
                if s == GROUPS + 3:
                    slots_at(7)
                if in_groups(s, 1):
                    conv(t + -1, 4)
                if in_groups(s, 3):
                    read(t + -3)
                if in_groups(s, 1):
                    conv(t + -1, 5)
                if in_groups(s, 0):
                    turn_x(t)
                if in_groups(s, 1):
                    conv(t + -1, 6)
                if in_groups(s, 2):
                    turn_m(t + -2)
                if s == GROUPS + 1:
                    slots_at(0)
                if s == GROUPS + 2:
                    slots_at(4)
                if in_groups(s, 0):
                    conv(t, 0)
                if in_groups(s, 4):
                    ranks(t + -4)
                if s == GROUPS + 2:
                    slots_at(5)
                if in_groups(s, 2):
                    queries(t + -2)
                    keys(t + -2)
                if s == GROUPS + 1:
                    slots_at(1)
                if in_groups(s, 0):
                    conv(t, 1)
                    conv(t, 2)
                if in_groups(s, 2):
                    scores(t + -2, 1)
                    scores(t + -2, 0)
                if in_groups(s, 1):
                    turn_h(t + -1)
                if s == GROUPS:
                    turn_table(0)
                if in_groups(s, 2):
                    values(t + -2)
                if in_groups(s, 3):
                    turn_xf(t + -3)
                if s == GROUPS + 1:
                    slots_at(2)
                if in_groups(s, 0):
                    conv(t, 3)

            run_part1(pe, step)
            slots_at(8)
            turn_table(1)
            pe.wait_ge(table_ready, 2)
            first_slots()

            run_part2(pe, step2, experts, 4, RING + 4)


_INS = ['x', 'L0_tok_weights', 'L0_attn_Wk', 'L0_attn_bk', 'L0_attn_Wq', 'L0_attn_bq', 'L0_attn_Wv', 'L0_attn_bv',
        'L0_ffn_W1', 'L0_ffn_b1', 'L0_ffn_W2', 'L0_ffn_b2', 'L0_ffn_Wg', 'L0_ffn_bg']


def kernel(**inputs):
    import numpy as _np
    import concourse.bacc as _bacc
    from concourse import mybir as _mybir
    from concourse.bass_utils import run_bass_kernel_spmd as _run

    nc = _bacc.Bacc("TRN2", target_bir_lowering=False, num_devices=1)
    arrays, args = {}, []
    for name in _INS:
        a = _np.ascontiguousarray(inputs[name])
        arrays[f"in_{name}_dram"] = a
        args.append(nc.dram_tensor(f"in_{name}_dram", a.shape, _mybir.dt.from_np(a.dtype), kind="ExternalInput").ap())
    b, t, c = inputs['x'].shape
    taps = inputs['L0_tok_weights'].shape[2]
    args.append(nc.dram_tensor("out_0_dram", (b, t - taps + 1, c), _mybir.dt.float32, kind="ExternalOutput").ap())
    audio_tower(nc, *args)
    r = _run(nc, [arrays], core_ids=[0])
    return r.results[0]["out_0_dram"]
```
